# Optimizing a Trainium2 kernel written in Bass

```python
import numpy as np
import jax
import jax.numpy as jnp

def _softmax(x, axis=-1):
    return jax.nn.softmax(x, axis=axis)

def _gelu(x):
    return jax.nn.gelu(x, approximate=True)

def _silu(x):
    return jax.nn.silu(x)

def _sigmoid(x):
    return jax.nn.sigmoid(x)

def _layernorm(x, axis=-1, eps=1e-05):
    m = jnp.mean(x, axis=axis, keepdims=True)
    v = jnp.var(x, axis=axis, keepdims=True)
    return (x - m) / jnp.sqrt(v + eps)

def _scatter_add(tgt, idx, src, axis=0):
    return tgt.at[idx].add(src)

def _segment_sum(src, seg, n):
    return jax.ops.segment_sum(src, seg, n)
kernel_name = 'mk_vit_tower_d1_tok_img768_r4_8af5f6'

def setup_inputs(seed: int=0):
    np.random.seed(seed)
    _w = jnp.asarray

    def _rec_inputs():
        import jax
        import jax.numpy as jnp
        _rk = jax.random.key(seed)
        x = -0.00016672 + 0.999947 * jax.random.normal(jax.random.fold_in(_rk, 1), (32, 3, 96, 96), jnp.float32)
        return x
    x = _rec_inputs()

    def _L0_tok_setup():
        import jax, jax.numpy as jnp
        import numpy as np
        B, C, H, W = (64, 3, 96, 96)
        P = 16
        EMBED = 192
        PATCH_DIM = C * P * P
        key = jax.random.key(seed)
        k1, k2, k3 = jax.random.split(key, 3)
        imgs = jax.random.normal(k1, (B, C, H, W), dtype=jnp.float32)
        bound = 1.0 / np.sqrt(PATCH_DIM)
        proj_w = jax.random.uniform(k2, (EMBED, PATCH_DIM), dtype=jnp.float32, minval=-bound, maxval=bound)
        proj_b = jax.random.uniform(k3, (EMBED,), dtype=jnp.float32, minval=-bound, maxval=bound)
        return {'imgs': imgs, 'proj_w': proj_w, 'proj_b': proj_b}
    _L0_tok_all = _L0_tok_setup()
    _L0_tok_in = {k: v for k, v in _L0_tok_all.items() if k in ('proj_w', 'proj_b')}
    del _L0_tok_all

    def _L0_attn_setup():
        import jax, jax.numpy as jnp
        import numpy as np
        QUAT = 4
        QMAX = float(2 ** QUAT - 1)
        HEADS = 12
        DIM_HEAD = 64

        def ste_round(x):
            return x + jax.lax.stop_gradient(jnp.round(x) - x)

        def fake_quant(q, s, z):
            zr = ste_round(z)
            return s * (jnp.clip(ste_round(q / s) + zr, 0.0, QMAX) - zr)
        key = jax.random.key(seed)
        k0, k1, k2, k3 = jax.random.split(key, 4)
        B, N, dim = (4, 512, 192)
        inner = HEADS * DIM_HEAD
        x = jax.random.normal(k0, (B, N, dim), jnp.float32)
        ww1 = jax.random.normal(k1, (3 * inner, dim), jnp.float32) * 0.02
        ww2 = jax.random.normal(k2, (dim, inner), jnp.float32) * 0.02
        bb2 = jax.random.normal(k3, (dim,), jnp.float32) * 0.02
        f = jnp.float32
        return {'x': x, 'ww1': ww1, 'ww2': ww2, 'bb2': bb2, 'sx1': f(0.27), 'zx1': f(8.0), 'sw1': f(0.0107), 'zw1': f(8.0), 'sq': f(0.15), 'zq': f(8.0), 'sk': f(0.15), 'zk': f(8.0), 'sa': f(1.0 / 15.0), 'za': f(0.0), 'sv': f(0.15), 'zv': f(8.0), 'sx2': f(0.05), 'zx2': f(8.0), 'sw2': f(0.0107), 'zw2': f(8.0)}
    _L0_attn_all = _L0_attn_setup()
    _L0_attn_in = {k: v for k, v in _L0_attn_all.items() if k in ('ww1', 'ww2', 'bb2', 'sx1', 'zx1', 'sw1', 'zw1', 'sq', 'zq', 'sk', 'zk', 'sa', 'za', 'sv', 'zv', 'sx2', 'zx2', 'sw2', 'zw2')}
    del _L0_attn_all

    def _L0_ffn_setup():
        import jax, jax.numpy as jnp
        import numpy as np
        B, T, E = (2, 256, 192)
        H = 768
        N_EXP = 4
        key = jax.random.key(seed)
        ks = jax.random.split(key, 8)
        s_e = 1.0 / np.sqrt(E)
        s_h = 1.0 / np.sqrt(H)
        return {'x': jax.random.normal(ks[0], (B, T, E), dtype=jnp.float32), 'Wg': jax.random.uniform(ks[1], (E, N_EXP), minval=-s_e, maxval=s_e, dtype=jnp.float32), 'bg': jax.random.uniform(ks[2], (N_EXP,), minval=-s_e, maxval=s_e, dtype=jnp.float32), 'W1': jax.random.uniform(ks[3], (N_EXP, E, H), minval=-s_e, maxval=s_e, dtype=jnp.float32), 'b1': jax.random.uniform(ks[4], (N_EXP, H), minval=-s_e, maxval=s_e, dtype=jnp.float32), 'W2': jax.random.uniform(ks[5], (N_EXP, H, E), minval=-s_h, maxval=s_h, dtype=jnp.float32), 'b2': jax.random.uniform(ks[6], (N_EXP, E), minval=-s_h, maxval=s_h, dtype=jnp.float32)}
    _L0_ffn_all = _L0_ffn_setup()
    _L0_ffn_in = {k: v for k, v in _L0_ffn_all.items() if k in ('Wg', 'bg', 'W1', 'b1', 'W2', 'b2')}
    del _L0_ffn_all
    return {'x': x, 'L0_tok_proj_w': _L0_tok_in['proj_w'], 'L0_tok_proj_b': _L0_tok_in['proj_b'], 'L0_attn_ww1': _L0_attn_in['ww1'], 'L0_attn_ww2': _L0_attn_in['ww2'], 'L0_attn_bb2': _L0_attn_in['bb2'], 'L0_attn_sx1': _L0_attn_in['sx1'], 'L0_attn_zx1': _L0_attn_in['zx1'], 'L0_attn_sw1': _L0_attn_in['sw1'], 'L0_attn_zw1': _L0_attn_in['zw1'], 'L0_attn_sq': _L0_attn_in['sq'], 'L0_attn_zq': _L0_attn_in['zq'], 'L0_attn_sk': _L0_attn_in['sk'], 'L0_attn_zk': _L0_attn_in['zk'], 'L0_attn_sa': _L0_attn_in['sa'], 'L0_attn_za': _L0_attn_in['za'], 'L0_attn_sv': _L0_attn_in['sv'], 'L0_attn_zv': _L0_attn_in['zv'], 'L0_attn_sx2': _L0_attn_in['sx2'], 'L0_attn_zx2': _L0_attn_in['zx2'], 'L0_attn_sw2': _L0_attn_in['sw2'], 'L0_attn_zw2': _L0_attn_in['zw2'], 'L0_ffn_Wg': _L0_ffn_in['Wg'], 'L0_ffn_bg': _L0_ffn_in['bg'], 'L0_ffn_W1': _L0_ffn_in['W1'], 'L0_ffn_b1': _L0_ffn_in['b1'], 'L0_ffn_W2': _L0_ffn_in['W2'], 'L0_ffn_b2': _L0_ffn_in['b2']}

def reference(x, L0_tok_proj_w, L0_tok_proj_b, L0_attn_ww1, L0_attn_ww2, L0_attn_bb2, L0_attn_sx1, L0_attn_zx1, L0_attn_sw1, L0_attn_zw1, L0_attn_sq, L0_attn_zq, L0_attn_sk, L0_attn_zk, L0_attn_sa, L0_attn_za, L0_attn_sv, L0_attn_zv, L0_attn_sx2, L0_attn_zx2, L0_attn_sw2, L0_attn_zw2, L0_ffn_Wg, L0_ffn_bg, L0_ffn_W1, L0_ffn_b1, L0_ffn_W2, L0_ffn_b2):
    import jax
    import jax.numpy as jnp

    def _L0_tok_ref(imgs, proj_w, proj_b):
        import jax, jax.numpy as jnp
        import numpy as np
        B, C, H, W = (64, 3, 96, 96)
        P = 16
        EMBED = 192
        PATCH_DIM = C * P * P
        b, c, h, w = imgs.shape
        p = P
        x = imgs.reshape(b, c, h // p, p, w // p, p)
        x = x.transpose(0, 2, 4, 1, 3, 5)
        x = x.reshape(b, h // p * (w // p), c * p * p)
        return jnp.einsum('bnd,ed->bne', x, proj_w) + proj_b

    def _L0_attn_ref(x, ww1, ww2, bb2, sx1, zx1, sw1, zw1, sq, zq, sk, zk, sa, za, sv, zv, sx2, zx2, sw2, zw2):
        import jax, jax.numpy as jnp
        import numpy as np
        QUAT = 4
        QMAX = float(2 ** QUAT - 1)
        HEADS = 12
        DIM_HEAD = 64

        def ste_round(x):
            return x + jax.lax.stop_gradient(jnp.round(x) - x)

        def fake_quant(q, s, z):
            zr = ste_round(z)
            return s * (jnp.clip(ste_round(q / s) + zr, 0.0, QMAX) - zr)
        B, N, dim = x.shape
        scale = DIM_HEAD ** (-0.5)
        qkv = fake_quant(x, sx1, zx1) @ fake_quant(ww1, sw1, zw1).T
        q, k, v = jnp.split(qkv, 3, axis=-1)

        def split_heads(t):
            return t.reshape(B, N, HEADS, DIM_HEAD).transpose(0, 2, 1, 3)
        q, k, v = map(split_heads, (q, k, v))
        dots = jnp.einsum('bhnd,bhmd->bhnm', fake_quant(q, sq, zq), fake_quant(k, sk, zk)) * scale
        a = jax.nn.softmax(dots, axis=-1)
        out = jnp.einsum('bhnm,bhmd->bhnd', fake_quant(a, sa, za), fake_quant(v, sv, zv))
        out = out.transpose(0, 2, 1, 3).reshape(B, N, HEADS * DIM_HEAD)
        return fake_quant(out, sx2, zx2) @ fake_quant(ww2, sw2, zw2).T + bb2

    def _L0_ffn_ref(x, Wg, bg, W1, b1, W2, b2):
        import jax, jax.numpy as jnp
        import numpy as np
        B, T, E = (2, 256, 192)
        H = 768
        N_EXP = 4
        gate_logits = jnp.einsum('bte,en->btn', x, Wg) + bg
        top = jnp.argmax(gate_logits, axis=-1)
        h = jax.nn.gelu(jnp.einsum('bte,neh->nbth', x, W1) + b1[:, None, None, :], approximate=False)
        y = jnp.einsum('nbth,nhe->nbte', h, W2) + b2[:, None, None, :]
        onehot = jax.nn.one_hot(top, N_EXP, dtype=x.dtype)
        out = jnp.einsum('nbte,btn->bte', y, onehot)
        return out
    h = _L0_tok_ref(x, L0_tok_proj_w, L0_tok_proj_b)
    h = h + _L0_attn_ref(_layernorm(h, axis=-1), L0_attn_ww1, L0_attn_ww2, L0_attn_bb2, L0_attn_sx1, L0_attn_zx1, L0_attn_sw1, L0_attn_zw1, L0_attn_sq, L0_attn_zq, L0_attn_sk, L0_attn_zk, L0_attn_sa, L0_attn_za, L0_attn_sv, L0_attn_zv, L0_attn_sx2, L0_attn_zx2, L0_attn_sw2, L0_attn_zw2)
    h = h + _L0_ffn_ref(_layernorm(h, axis=-1), L0_ffn_Wg, L0_ffn_bg, L0_ffn_W1, L0_ffn_b1, L0_ffn_W2, L0_ffn_b2)
    return h

_drawn_inputs = setup_inputs


def setup_inputs(seed=0):
    import zlib

    import numpy as np

    out = dict(_drawn_inputs(seed))
    spreads = {}
    factors = {}
    for name, (base, spread) in spreads.items():
        noise = np.random.default_rng([zlib.crc32(name.encode()), seed]).standard_normal(out[name].shape)
        drawn = base * np.exp(spread * noise) if base else spread * noise
        out[name] = jnp.asarray(drawn.astype(out[name].dtype))
    for name, factor in factors.items():
        out[name] = (out[name] * factor).astype(out[name].dtype)
    return out
```

```python
from contextlib import ExitStack

import concourse.bass as bass
from concourse import mybir

F32 = mybir.dt.float32
BF16 = mybir.dt.bfloat16
F16 = mybir.dt.float16
I16 = mybir.dt.int16
I32 = mybir.dt.int32
U32 = mybir.dt.uint32
ALU = mybir.AluOpType
ACT = mybir.ActivationFunctionType
AX = mybir.AxisListType

P = 128
ROUND = 1.5 * 2.0 ** 23
QMAX = 15.0
EPS = 1e-5
WSCALE = 64.0
YB = 4
NCONST = 3 + 4 + 3 + 4 + 12
X1, W1Q, QQ, KQ, AQ, VQ, X2, W2Q = range(8)


def vit_kernel(nc, patches_d, proj_w_d, proj_b_d, quant_d, ww1_d, ww2_d, bb2_d,
               gate_w_d, gate_b_d, w1_d, b1_d, w2_d, b2_d, out_d):
    _, TT, KE, _ = patches_d.shape
    T = TT * P
    E = proj_w_d.shape[2]
    EC = E // 2
    NTOK = 36
    IMGS = T // NTOK
    PAIRS = IMGS // 2
    HEADS, DH = 12, 64
    INNER = HEADS * DH
    HB = INNER // P
    _, NEXP, HM = b1_d.shape
    HID = HM * P
    CH = 288
    CI = CH // NTOK
    CHUNKS = T // CH
    PPC = PAIRS // CHUNKS
    HT = HEADS * NTOK
    SLOT_TILES = (T + NEXP * (P - 1)) // P
    SLOTS = SLOT_TILES * P
    ROW = 2 * E + 4
    QG, VG = HB // 2, PPC

    with ExitStack() as ctx:
        def sb(name, shape, dt=F32):
            return ctx.enter_context(nc.sbuf_tensor(name, shape, dt))

        def sem(name):
            return ctx.enter_context(nc.semaphore(name))

        def psum(name, shape):
            return ctx.enter_context(nc.psum_tensor(name, shape, F32))

        lin_bank = [psum(f"lin_bank{i}", [P, 2, 512]) for i in range(2)]
        score_bank = psum("score_bank", [P, 512])
        probT_bank = psum("probT_bank", [P, 512])
        head_bank = psum("head_bank", [P, 2, 512])
        emb_bank = [head_bank[:, 0], head_bank[:, 1], lin_bank[1][:, 0], lin_bank[1][:, 1]]
        up_bank = [lin_bank[i // 2][:, i % 2] for i in range(4)]
        slotT_bank = [score_bank[:], probT_bank[:]]
        down_bank = [head_bank[:, 0], head_bank[:, 1]]

        patches = sb("patches", [P, TT, KE, P])
        proj_w = sb("proj_w", [P, KE, E])
        proj_b = sb("proj_b", [P, E])
        bb2 = sb("bb2", [P, E])
        quant = sb("quant", [P, 16])
        early = sb("early", [P, 6 * INNER])
        ww1 = early[0:EC].rearrange("p (c n) -> p c n", c=2)
        ww1q = sb("ww1q", [EC, 2, 3 * INNER], BF16)
        ww2 = sb("ww2", [P, HB, E])
        ww2q = sb("ww2q", [P, HB, E], BF16)
        wint = sb("wint", [P, 2, INNER], I16)
        inv = sb("inv", [P, 8])
        zr = sb("zr", [P, 8])
        lo = sb("lo", [P, 8])
        hi = sb("hi", [P, 8])
        fac = sb("fac", [P, 8])
        sxw, rq, rk, rv, cexp, ro, so, tmp = (fac[:, i:i + 1] for i in range(8))
        ident = sb("ident", [P, P])
        identb = sb("identb", [P, P], BF16)
        identh = sb("identh", [P, P], F16)
        before = sb("before", [P, P], BF16)
        ones = sb("ones", [P, P], BF16)
        row = sb("row", [P, TT, ROW])
        row16 = row[:].rearrange("p t n -> p (t n)").bitcast(F16).rearrange("p (t n) -> p t n", t=TT)
        blank = sb("blank", [P, ROW])
        stats = sb("stats", [P, 2, 6])
        mv = sb("mv", [P, TT, 2])
        veps = sb("veps", [P, TT])
        rstd = sb("rstd", [P, TT])
        rscale = sb("rscale", [P, TT])
        nhalf = sb("nhalf", [P, 1])
        xint = sb("xint", [P, 2, E], I16)
        xq = sb("xq", [P, TT, E], BF16)
        xqT = sb("xqT", [EC, 2, IMGS, DH], BF16)
        qkint = sb("qkint", [P, 2 * HB, CH], I16)
        q = sb("q", [P, 2, HB, CH], BF16)
        k = sb("k", [P, 2, HB, CI, 2, NTOK], BF16)
        vint = sb("vint", [P, 2, INNER], I16)
        v = sb("v", [P, 2 * PPC, INNER], BF16)
        mx = sb("mx", [P, 2, HEADS])
        den = sb("den", [P, 2, HEADS])
        dens = sb("dens", [P, 2, HEADS])
        rden = sb("rden", [P, 2, HEADS])
        dif = sb("dif", [P, 2, HT])
        ex = sb("ex", [P, 2, HT])
        aint = sb("aint", [P, 2, HT], I16)
        aq = sb("aq", [P, 2, HT], BF16)
        aT = sb("aT", [P, 2, HT], BF16)
        oint = sb("oint", [P, 2, HB, 4 * NTOK], I16)
        oT = sb("oT", [P, HB, T], BF16)
        xn = sb("xn", [P, 2, E])
        xnT = sb("xnT", [EC, 2, 2, P])
        gate_w = sb("gate_w", [EC, 2, NEXP])
        gate_b = sb("gate_b", [P, NEXP])
        prio = sb("prio", [P, NEXP])
        earlier = sb("earlier", [P, NEXP, NEXP])
        tile_no = sb("tile_no", [P, SLOT_TILES])
        logit = sb("logit", [P, TT, NEXP])
        isbest = sb("isbest", [P, TT, NEXP])
        best = sb("best", [P, TT])
        onehot = sb("onehot", [P, TT + 1, NEXP], BF16)
        ntile = sb("ntile", [P, NEXP])
        first = sb("first", [P, NEXP])
        prod = sb("prod", [P, NEXP, NEXP])
        place = sb("place", [P, TT, NEXP])
        slot = sb("slot", [P, TT], I32)
        started = sb("started", [P, SLOT_TILES, NEXP])
        expert = sb("expert", [P, SLOT_TILES], I32)
        expert_f = sb("expert_f", [P, SLOT_TILES])
        slot_f = sb("slot_f", [P, TT])
        b1 = sb("b1", [P, NEXP, HM])
        b2 = sb("b2", [P, NEXP, E])
        w1 = sb("w1", [EC, NEXP, 2, 2, HID], F16)
        w2 = early[:].bitcast(F16).rearrange("p (e s m n) -> p e s m n", e=NEXP, s=2, m=HM)
        warm = sb("warm", [1, 1])
        flat = patches[:].rearrange("p t k n -> p (t k n)")
        w1f = flat[0:EC, 0:NEXP * 2 * HID].rearrange("p (e c n) -> p e c n", e=NEXP, c=2)
        w2f = flat[:, 0:NEXP * 2 * HID].rearrange("p (e n) -> p e n", e=NEXP)[:, :, 0:HM * E].rearrange(
            "p e (m n) -> p e m n", m=HM)
        nx = SLOT_TILES * ROW
        xs = flat[:, 0:nx].rearrange("p (j n) -> p j n", n=ROW)
        xs16 = flat[:, 0:nx].bitcast(F16).rearrange("p (j n) -> p j n", n=2 * ROW)
        g = flat[:, nx:nx + 2 * HID].rearrange("p (b m n) -> p b m n", b=2, m=HM)
        late = k[:].rearrange("p b m i h n -> p (b m i h n)").bitcast(F32)
        gs = late[:, 0:2 * HID].bitcast(F16).rearrange("p (b s m n) -> p b s m n", b=2, s=2, m=HM)
        x0 = 2 * HID
        xT = late[0:EC, x0:x0 + 3 * 2 * P].bitcast(F16).rearrange("p (b s n) -> p b s n", b=3, s=4)
        y0 = x0 + 3 * 2 * P
        yo = late[:, y0:y0 + YB * E].rearrange("p (b n) -> p b n", b=YB)
        hres = late[:, y0 + YB * E:y0 + (YB + 2) * E].rearrange("p (b n) -> p b n", b=2)
        slots_d = nc.dram_tensor("slots", (SLOTS, ROW), F32).ap()

        (quant_in, proj_in, bias_in, bb2_in, ww1_in, ww2_in, gate_in, w1_in, b12_in, blank_out,
         scattered) = map(sem, (
             "quant_in", "proj_in", "bias_in", "bb2_in", "ww1_in", "ww2_in", "gate_in", "w1_in", "b12_in",
             "blank_out", "scattered"))
        stored = [sem(f"stored{b}") for b in range(YB)]
        w2_in = [sem(f"w2_in{e}") for e in range(NEXP)]
        patch_in = [sem(f"patch_in{t}") for t in range(TT)]
        xs_in = [sem(f"xs_in{j}") for j in range(SLOT_TILES)]
        pool_step, ident_ok, pad_ok, kpad_ok, blank_ok, const_ok, setup, scales_ok, psum_clear = map(sem, (
            "pool_step", "ident_ok", "pad_ok", "kpad_ok", "blank_ok", "const_ok", "setup", "scales_ok", "psum_clear"))
        w_int, w_quant, emb_ps, h_ok, stat_ok, aggr_ok, var_ok, rstd_ok, rscale_ok, norm_ok, xq_ok = map(sem, (
            "w_int", "w_quant", "emb_ps", "h_ok", "stat_ok", "aggr_ok", "var_ok", "rstd_ok", "rscale_ok",
            "norm_ok", "xq_ok"))
        hb_ok, xqT_ps, xqT_ok = map(sem, ("hb_ok", "xqT_ps", "xqT_ok"))
        lin_ps, lin_int, q_ok, k_ok, v_ok = map(sem, ("lin_ps", "lin_int", "q_ok", "k_ok", "v_ok"))
        s_ps, mx_ok, dif_ok, ex_ok, den_ok, dens_ok, rden_ok, aint_ok, aq_ok = map(sem, (
            "s_ps", "mx_ok", "dif_ok", "ex_ok", "den_ok", "dens_ok", "rden_ok", "aint_ok", "aq_ok"))
        aT_ps, aT_ok, o_ps, o_int, o_ok = map(sem, ("aT_ps", "aT_ok", "o_ps", "o_int", "o_ok"))
        pr_ps, h2_ok, xn_ok, xhi_ok, xlo_ok, xnT_ps, xnT_ok, gate_ps = map(sem, (
            "pr_ps", "h2_ok", "xn_ok", "xhi_ok", "xlo_ok", "xnT_ps", "xnT_ok", "gate_ps"))
        whi_ok, wlo_ok, route, onehot_ok, count_ps, slot_ok, expert_ok = map(sem, (
            "whi_ok", "wlo_ok", "route", "onehot_ok", "count_ps", "slot_ok", "expert_ok"))
        slotT_ps, slotT_ok, up_ps, g_ok, ghi_ok, glo_ok, down_ps, res_ok, y_ok = map(sem, (
            "slotT_ps", "slotT_ok", "up_ps", "g_ok", "ghi_ok", "glo_ok", "down_ps", "res_ok", "y_ok"))

        STEPS = PAIRS + 7

        def lin_groups(i):
            if i == -1:
                return [("q", 0, n) for n in range(QG)] + [("k", 0, n) for n in range(QG)]
            out = []
            c, r = divmod(i, PPC)
            if r == 0 and c < CHUNKS:
                out += [("v", c, n) for n in range(0 if c == 0 else VG // 2, VG)]
            if c + 1 < CHUNKS:
                if r == 1:
                    out += [("q", c + 1, n) for n in range(QG)]
                if r == 2:
                    out += [("k", c + 1, n) for n in range(QG)]
                if r == 3:
                    out += [("v", c + 1, n) for n in range(VG // 2)]
            return out

        def tiles_at(i, delay):
            n = i - delay - 4
            if n < 0 or n % 2 or n // 2 >= PAIRS // 2:
                return []
            n //= 2
            done = [4 * NTOK * x // P for x in (n, n + 1)]
            return list(range(*done))

        lin_no, lin_order = {}, []
        ring = []
        for i in range(-1, STEPS):
            for x in lin_groups(i):
                lin_no[x] = len(lin_order)
                lin_order.append(x)
                ring.append(("lin", lin_no[x]))
            ring += [("proj", t) for t in tiles_at(i, 0)]
            ring += [("xnT", t) for t in tiles_at(i, 3)]
        ring_no = {x: n for n, x in enumerate(ring)}

        SPLITS = [(1, e, c) for e in range(NEXP) for c in range(2)] + [(2, e, c) for e in range(NEXP) for c in range(2)]

        def split_views(n):
            which, e, c = SPLITS[n]
            if which == 1:
                return w1f[:, e, c], w1[:, e, 0, c], w1[:, e, 1, c]
            ms = slice(c * HM // 2, (c + 1) * HM // 2)
            return w2f[:, e, ms], w2[:, e, 0, ms], w2[:, e, 1, ms]

        WCH = [(s, c) for s in range(3) for c in range(2)] + [(3, c) for c in range(2)]

        def weight_views(n):
            s, c = WCH[n]
            if s < 3:
                cols = slice(s * INNER, (s + 1) * INNER)
                return W1Q, ww1[:, c, cols], wint[0:EC, n % 2], ww1q[:, c, cols]
            ms = slice(c * HB // 2, (c + 1) * HB // 2)
            return W2Q, ww2[:, ms], wint[:, n % 2, 0:HB // 2 * E].rearrange("p (m n) -> p m n", n=E), ww2q[:, ms]

        def heads(x):
            return x.rearrange("p (h n) -> p h n", n=NTOK)

        block = ctx.enter_context(nc.Block())

        @block.sync
        def _(sp):
            sp.dma_start(quant[:], quant_d.partition_broadcast(P)).then_inc(quant_in, 16)
            sp.dma_start(proj_w[:], proj_w_d).then_inc(proj_in, 16)
            for t in range(TT):
                sp.dma_start(patches[:, t], patches_d[:, t]).then_inc(patch_in[t], 16)
                if t == 0:
                    sp.dma_start(proj_b[:], proj_b_d.partition_broadcast(P)).then_inc(bias_in, 16)
                    sp.dma_start(bb2[:], bb2_d.partition_broadcast(P)).then_inc(bb2_in, 16)
                if t == 2:
                    sp.dma_start(ww1, ww1_d).then_inc(ww1_in, 16)
            sp.dma_start(ww2[:], ww2_d).then_inc(ww2_in, 16)
            sp.dma_start(gate_w[:], gate_w_d).then_inc(gate_in, 16)
            sp.dma_start(gate_b[:], gate_b_d.partition_broadcast(P)).then_inc(gate_in, 16)
            sp.wait_ge(emb_ps, TT)
            sp.dma_start(w1f, w1_d).then_inc(w1_in, 16)
            sp.dma_start(b1[:], b1_d).then_inc(b12_in, 16)
            sp.dma_start(b2[:], b2_d.rearrange("e n -> (e n)").partition_broadcast(P)).then_inc(b12_in, 16)
            sp.wait_ge(blank_ok, 2)
            for j in range(SLOT_TILES):
                sp.dma_start(slots_d[j * P:(j + 1) * P, :], blank[:]).then_inc(blank_out, 16)
            for e in range(NEXP):
                sp.wait_ge(wlo_ok, 2 * e + 2)
                sp.dma_start(w2f[:, e], w2_d[:, e]).then_inc(w2_in[e], 16)
            sp.wait_ge(wlo_ok, len(SPLITS))
            sp.wait_ge(scattered, 16 * TT)
            for j in range(SLOT_TILES):
                sp.dma_start(xs[:, j], slots_d[j * P:(j + 1) * P, :]).then_inc(xs_in[j], 16)

        @block.gpsimd
        def _(pool):
            gp = nc.gpsimd
            steps = [0]

            def step(ins):
                steps[0] += 1
                ins.then_inc(pool_step, 1)
                pool.wait_ge(pool_step, steps[0])

            step(gp.memset(ident[:], 0.0))
            step(gp.affine_select(out=ident[:], in_=ident[:], compare_op=ALU.not_equal, fill=1.0, base=0,
                                  pattern=[[-1, P]], channel_multiplier=1))
            gp.tensor_copy(identb[:], ident[:]).then_inc(ident_ok, 1)
            gp.tensor_copy(identh[:], ident[:]).then_inc(ident_ok, 1)
            gp.memset(nhalf[:], -0.5).then_inc(ident_ok, 1)
            gp.memset(xqT[:], 0.0).then_inc(pad_ok, 1)
            pool.wait_ge(ident_ok, 3)
            for t in range(3):
                pool.wait_ge(var_ok, t + 1)
                gp.tensor_tensor(rstd[:, t:t + 1], veps[:, t:t + 1], nhalf[:], ALU.pow).then_inc(rstd_ok, 1)
            gp.memset(k[:].rearrange("p b m i h n -> p (b m i h n)").bitcast(U32), 0).then_inc(kpad_ok, 1)
            for t in range(3, TT):
                pool.wait_ge(var_ok, t + 1)
                gp.tensor_tensor(rstd[:, t:t + 1], veps[:, t:t + 1], nhalf[:], ALU.pow).then_inc(rstd_ok, 1)
            pool.wait_ge(bb2_in, 16)
            for t in range(TT):
                pool.wait_ge(norm_ok, t + 1)
                gp.tensor_tensor(row[:, t, 0:E], row[:, t, 0:E], bb2[:], ALU.add).then_inc(hb_ok, 1)
            step(gp.memset(blank[:, 0:2 * E], 0.0))
            gp.iota(blank[:, 2 * E:ROW].bitcast(I32), pattern=[[0, 4]], base=T, channel_multiplier=1).then_inc(blank_ok, 1)
            gp.iota(row[:, :, 2 * E:ROW].bitcast(I32), pattern=[[P, TT], [0, 4]], base=0,
                    channel_multiplier=1).then_inc(blank_ok, 1)
            step(gp.memset(before[:], 1.0))
            gp.affine_select(out=before[:], in_=before[:], compare_op=ALU.is_gt, fill=0.0, base=0,
                             pattern=[[1, P]], channel_multiplier=-1).then_inc(const_ok, 1)
            gp.memset(ones[:], 1.0).then_inc(const_ok, 1)
            gp.memset(onehot[:, TT], 0.0).then_inc(const_ok, 1)
            for e in range(NEXP):
                gp.memset(prio[:, e:e + 1], float(NEXP - e)).then_inc(const_ok, 1)
                if e:
                    gp.memset(earlier[:, e, 0:e], 1.0).then_inc(const_ok, 1)
                gp.memset(earlier[:, e, e:], 0.0).then_inc(const_ok, 1)
            for j in range(SLOT_TILES):
                gp.memset(tile_no[:, j:j + 1], float(j)).then_inc(const_ok, 1)
            for t in range(TT):
                pool.wait_ge(var_ok, TT + t + 1)
                gp.tensor_tensor(rstd[:, t:t + 1], veps[:, t:t + 1], nhalf[:], ALU.pow).then_inc(rstd_ok, 1)
            pool.wait_ge(blank_out, 16 * SLOT_TILES)
            pool.wait_ge(xlo_ok, TT)
            pool.wait_ge(xhi_ok, TT)
            pool.wait_ge(slot_ok, 1)
            for t in range(TT):
                gp.indirect_dma_start(out=slots_d, out_offset=bass.IndirectOffsetOnAxis(ap=slot[:, t:t + 1], axis=0),
                                      in_=row[:, t, :], in_offset=None,
                                      bounds_check=SLOTS - 1, oob_is_err=False).then_inc(scattered, 16)
            for j in range(SLOT_TILES):
                pool.wait_ge(y_ok, j + 1)
                gp.indirect_dma_start(out=out_d, out_offset=bass.IndirectOffsetOnAxis(
                                          ap=xs[:, j, 2 * E:2 * E + 1].bitcast(I32), axis=0),
                                      in_=yo[:, j % YB, :], in_offset=None,
                                      bounds_check=T - 1, oob_is_err=False).then_inc(stored[j % YB], 16)
            for b in range(YB):
                pool.wait_ge(stored[b], 16 * (SLOT_TILES // YB))

        @block.scalar
        def _(act):
            a = nc.scalar

            def weights(n):
                s, w, wi, _ = weight_views(n)
                if n >= 2:
                    act.wait_ge(w_quant, n - 1)
                a.activation(wi, w, ACT.Copy, scale=inv[0:w.shape[0], s:s + 1]).then_inc(w_int, 1)

            def tokens_T(c):
                act.wait_ge(xqT_ps, c + 1)
                off = c * CH % P
                src = score_bank[0:EC, :].bitcast(BF16)[:, 0:2 * 3 * P].rearrange("p (c n) -> p c n", c=2)
                a.copy(xqT[:, :, c * CI:(c + 1) * CI, 0:NTOK],
                       src[:, :, off:off + CH].rearrange("p c (i n) -> p c i n", n=NTOK)).then_inc(xqT_ok, 1)

            def linear(x):
                kind, c, n = x
                j = lin_no[x]
                bank = lin_bank[ring_no[("lin", j)] % 2]
                act.wait_ge(lin_ps, j + 1)
                if kind == "v":
                    p = c * PPC + n
                    if p >= 2:
                        act.wait_ge(v_ok, p - 1)
                    a.activation(vint[:, p % 2].rearrange("p (s n) -> p s n", s=2), bank[:, :, 0:INNER // 2],
                                 ACT.Copy, scale=rv).then_inc(lin_int, 1)
                    return
                m = 2 * n
                if kind == "k":
                    m += HB
                if c >= 1 and n == 0:
                    act.wait_ge(q_ok if kind == "q" else k_ok, c if kind == "q" else 2 * c)
                a.activation(qkint[:, m:m + 2], bank[:, :, 0:CH], ACT.Copy,
                             scale=rq if kind == "q" else rk).then_inc(lin_int, 1)

            act.wait_ge(scales_ok, 1)
            act.wait_ge(ww1_in, 16)
            act.wait_ge(pad_ok, 1)
            for n in range(len(WCH)):
                if n == 6:
                    act.wait_ge(ww2_in, 16)
                weights(n)
                if n in (5, 7):
                    tokens_T((n - 5) // 2)
            for x in lin_groups(-1):
                linear(x)
            for c in range(2, CHUNKS):
                tokens_T(c)
            for i in range(STEPS):
                if i < PAIRS:
                    b = i % 2
                    act.wait_ge(dif_ok, i + 1)
                    if i >= 2:
                        act.wait_ge(aint_ok, i - 1)
                    a.activation(ex[:, b], dif[:, b], ACT.Exp, scale=cexp).then_inc(ex_ok, 1)
                for x in lin_groups(i):
                    linear(x)
                p = i - 2
                if 0 <= p < PAIRS:
                    act.wait_ge(o_ps, p + 1)
                    if p >= 4 and p % 2 == 0:
                        act.wait_ge(o_ok, p // 2 - 1)
                    dst = oint[:, p // 2 % 2, :, (p % 2) * 2 * NTOK:(p % 2 + 1) * 2 * NTOK]
                    a.activation(dst.rearrange("p m (r n) -> p r m n", r=2),
                                 head_bank[:, :, 0:HB * NTOK].rearrange("p r (m n) -> p r m n", m=HB),
                                 ACT.Copy, scale=ro).then_inc(o_int, 1)
                for t in tiles_at(i, 3):
                    act.wait_ge(xnT_ps, t + 1)
                    if t >= 2:
                        act.wait_ge(gate_ps, t - 1)
                    a.copy(xnT[:, t % 2], lin_bank[ring_no[("xnT", t)] % 2][0:EC, 0, 0:2 * P].rearrange(
                        "p (c n) -> p c n", c=2)).then_inc(xnT_ok, 1)
                if 1 <= i <= len(SPLITS):
                    if i == 1:
                        act.wait_ge(w1_in, 16)
                    which, e, _ = SPLITS[i - 1]
                    if which == 2:
                        act.wait_ge(w2_in[e], 16)
                    w, whi, _ = split_views(i - 1)
                    a.activation(whi, w, ACT.Copy, scale=WSCALE).then_inc(whi_ok, 1)
                for t in tiles_at(i, 2):
                    act.wait_ge(xn_ok, t + 1)
                    a.copy(row16[:, t, 2 * E:3 * E], xn[:, t % 2]).then_inc(xhi_ok, 1)
                p = i - 1
                if 0 <= p < PAIRS:
                    act.wait_ge(aT_ps, p + 1)
                    if p >= 2:
                        act.wait_ge(o_ps, p - 1)
                    a.copy(aT[:, p % 2], probT_bank[:, 0:HT // 2].bitcast(BF16)).then_inc(aT_ok, 1)
            act.wait_ge(const_ok, 1)
            a.activation(warm[:], nhalf[0:1], ACT.Gelu)
            act.wait_ge(b12_in, 32)
            act.wait_ge(expert_ok, 1)
            for j in range(SLOT_TILES):
                e = act.value_load(expert[0:1, j:j + 1], min_val=0, max_val=NEXP - 1)
                for m in range(HM):
                    n = j * HM + m
                    act.wait_ge(up_ps, n + 1)
                    if j >= 2 and m == 0:
                        act.wait_ge(glo_ok, j - 1)
                    a.activation(g[:, j % 2, m], up_bank[n % 4][:, 0:P], ACT.Gelu, scale=1.0 / WSCALE,
                                 bias=b1[:, bass.ds(e, 1), m]).then_inc(g_ok, 1)

        @block.vector
        def _(dve):
            d = nc.vector
            steps = [0]

            def step(ins):
                steps[0] += 1
                ins.then_inc(setup, 1)
                dve.wait_ge(setup, steps[0])

            def mul(out, x, y):
                step(d.tensor_tensor(out, x, y, ALU.mult))

            d.memset(score_bank[:], 0.0).then_inc(psum_clear, 1)
            d.memset(probT_bank[:], 0.0).then_inc(psum_clear, 1)
            dve.wait_ge(quant_in, 16)
            scl, zero = quant[:, 0:8], quant[:, 8:16]
            step(d.reciprocal(inv[:], scl))
            step(d.tensor_scalar(zr[:], zero, ROUND, ROUND, ALU.add, ALU.subtract))
            step(d.tensor_scalar(lo[:], zr[:], -1.0, None, ALU.mult))
            step(d.tensor_scalar(hi[:], zr[:], -1.0, QMAX, ALU.mult, ALU.add))
            mul(sxw, scl[:, X1:X1 + 1], scl[:, W1Q:W1Q + 1])
            mul(rq, sxw, inv[:, QQ:QQ + 1])
            mul(rk, sxw, inv[:, KQ:KQ + 1])
            mul(rv, sxw, inv[:, VQ:VQ + 1])
            mul(tmp, scl[:, QQ:QQ + 1], scl[:, KQ:KQ + 1])
            step(d.tensor_scalar(cexp, tmp, DH ** -0.5, None, ALU.mult))
            mul(tmp, scl[:, AQ:AQ + 1], scl[:, VQ:VQ + 1])
            mul(ro, tmp, inv[:, X2:X2 + 1])
            d.tensor_tensor(so, scl[:, X2:X2 + 1], scl[:, W2Q:W2Q + 1], ALU.mult).then_inc(scales_ok, 1)
            dve.wait_ge(scales_ok, 1)

            def clip(out, x, s, n=P, base=0):
                return d.tensor_scalar(out, x, lo[base:base + n, s:s + 1], hi[base:base + n, s:s + 1],
                                       ALU.max, ALU.min)

            def weights(n):
                s, w, wi, wq = weight_views(n)
                dve.wait_ge(w_int, n + 1)
                clip(wq, wi, s, w.shape[0]).then_inc(w_quant, 1)

            def measure(t, n):
                d.bn_stats(stats[:, n % 2], row[:, t, 0:E]).then_inc(stat_ok, 1)
                dve.wait_ge(stat_ok, n + 1)
                d.bn_aggr(mv[:, t], stats[:, n % 2]).then_inc(aggr_ok, 1)
                dve.wait_ge(aggr_ok, n + 1)
                d.tensor_scalar(veps[:, t:t + 1], mv[:, t, 1:2], EPS, None, ALU.add).then_inc(var_ok, 1)

            def quant_tokens(t):
                dve.wait_ge(rstd_ok, t + 1)
                d.tensor_tensor(rscale[:, t:t + 1], rstd[:, t:t + 1], inv[:, X1:X1 + 1], ALU.mult).then_inc(rscale_ok, 1)
                dve.wait_ge(rscale_ok, t + 1)
                d.tensor_scalar(xint[:, t % 2], row[:, t, 0:E], mv[:, t, 0:1], rscale[:, t:t + 1],
                                ALU.subtract, ALU.mult).then_inc(norm_ok, 1)
                dve.wait_ge(norm_ok, t + 1)
                clip(xq[:, t], xint[:, t % 2], X1).then_inc(xq_ok, 1)

            def linear(x):
                kind, c, n = x
                dve.wait_ge(lin_int, lin_no[x] + 1)
                if kind == "q":
                    if c >= 2:
                        dve.wait_ge(s_ps, (c - 1) * PPC)
                    clip(q[:, c % 2], qkint[:, 0:HB], QQ).then_inc(q_ok, 1)
                elif kind == "k":
                    if c >= 2:
                        dve.wait_ge(s_ps, (c - 1) * PPC)
                    if c == 0:
                        dve.wait_ge(kpad_ok, 1)
                    for hp in range(2):
                        rows = slice(DH * hp, DH * hp + DH)
                        clip(k[rows, c % 2, :, :, hp], qkint[rows, HB:2 * HB].rearrange("p m (i n) -> p m i n", n=NTOK),
                             KQ, DH, DH * hp).then_inc(k_ok, 1)
                else:
                    p = c * PPC + n
                    if p >= 2 * PPC:
                        dve.wait_ge(o_ps, p - 2 * PPC + 1)
                    clip(v[:, p % (2 * PPC)], vint[:, p % 2], VQ).then_inc(v_ok, 1)

            def clips(i):
                for x in lin_groups(i):
                    if x[0] == "v" or x[2] == QG - 1:
                        linear(x)

            for t in range(TT):
                dve.wait_ge(emb_ps, t + 1)
                if t == 0:
                    dve.wait_ge(bias_in, 16)
                d.tensor_tensor(row[:, t, 0:E], emb_bank[t % 4][:, 0:E], proj_b[:], ALU.add).then_inc(h_ok, 1)
                dve.wait_ge(h_ok, t + 1)
                measure(t, t)
                if t >= 1:
                    quant_tokens(t - 1)
                if t >= 2 and t - 2 < len(WCH):
                    weights(t - 2)
            quant_tokens(TT - 1)
            for n in range(TT - 2, len(WCH)):
                weights(n)
            clips(-1)

            for i in range(STEPS):
                if i < PAIRS:
                    b = i % 2
                    dve.wait_ge(s_ps, i + 1)
                    d.tensor_reduce(mx[:, b], heads(score_bank[:, 0:HT]), AX.X, ALU.max).then_inc(mx_ok, 1)
                    dve.wait_ge(mx_ok, i + 1)
                    if i >= 2:
                        dve.wait_ge(ex_ok, i - 1)
                    d.tensor_tensor(heads(dif[:, b]), heads(score_bank[:, 0:HT]),
                                    mx[:, b].unsqueeze(2).to_broadcast([P, HEADS, NTOK]),
                                    ALU.subtract).then_inc(dif_ok, 1)
                if i >= 1:
                    clips(i - 1)
                n = i - 4
                if n >= 0 and n % 2 == 0 and n // 2 < PAIRS // 2:
                    n //= 2
                    dve.wait_ge(o_int, 2 * n + 2)
                    clip(oT[:, :, n * 4 * NTOK:(n + 1) * 4 * NTOK], oint[:, n % 2], X2).then_inc(o_ok, 1)
                p = i - 1
                if 0 <= p < PAIRS:
                    b = p % 2
                    dve.wait_ge(ex_ok, p + 1)
                    d.tensor_reduce(den[:, b], heads(ex[:, b]), AX.X, ALU.add).then_inc(den_ok, 1)
                    dve.wait_ge(den_ok, p + 1)
                    d.tensor_scalar(dens[:, b], den[:, b], scl[:, AQ:AQ + 1], None, ALU.mult).then_inc(dens_ok, 1)
                    dve.wait_ge(dens_ok, p + 1)
                    d.reciprocal(rden[:, b], dens[:, b]).then_inc(rden_ok, 1)
                    dve.wait_ge(rden_ok, p + 1)
                    d.tensor_tensor(heads(aint[:, b]), heads(ex[:, b]),
                                    rden[:, b].unsqueeze(2).to_broadcast([P, HEADS, NTOK]),
                                    ALU.mult).then_inc(aint_ok, 1)
                    dve.wait_ge(aint_ok, p + 1)
                    if p >= 2:
                        dve.wait_ge(aT_ps, p - 1)
                    clip(aq[:, b], aint[:, b], AQ).then_inc(aq_ok, 1)
                for t in tiles_at(i, 3):
                    dve.wait_ge(xhi_ok, t + 1)
                    d.tensor_tensor(row16[:, t, 3 * E:4 * E], xn[:, t % 2], row16[:, t, 2 * E:3 * E],
                                    ALU.subtract).then_inc(xlo_ok, 1)
                for t in tiles_at(i, 1):
                    dve.wait_ge(pr_ps, t + 1)
                    dve.wait_ge(hb_ok, t + 1)
                    d.scalar_tensor_tensor(row[:, t, 0:E], lin_bank[ring_no[("proj", t)] % 2][:, 0, 0:E], so,
                                           row[:, t, 0:E], ALU.mult, ALU.add).then_inc(h2_ok, 1)
                    dve.wait_ge(h2_ok, t + 1)
                    measure(t, TT + t)
                for t in tiles_at(i, 2):
                    dve.wait_ge(rstd_ok, TT + t + 1)
                    if t >= 2:
                        dve.wait_ge(xnT_ps, t - 1)
                    d.tensor_scalar(xn[:, t % 2], row[:, t, 0:E], mv[:, t, 0:1], rstd[:, t:t + 1],
                                    ALU.subtract, ALU.mult).then_inc(xn_ok, 1)
                if 2 <= i < 2 + len(SPLITS):
                    w, whi, wlo = split_views(i - 2)
                    dve.wait_ge(whi_ok, i - 1)
                    d.scalar_tensor_tensor(wlo, w, WSCALE, whi, ALU.mult, ALU.subtract).then_inc(wlo_ok, 1)

            routed = [0]

            def rstep(ins):
                routed[0] += 1
                ins.then_inc(route, 1)
                dve.wait_ge(route, routed[0])

            def each_expert(x, n=TT):
                return x.unsqueeze(2).to_broadcast([P, n, NEXP])

            def each_tile(x, n=TT):
                return x.unsqueeze(1).to_broadcast([P, n, NEXP])

            dve.wait_ge(gate_in, 32)
            dve.wait_ge(const_ok, NCONST)
            dve.wait_ge(gate_ps, TT)
            rstep(d.tensor_tensor(logit[:], score_bank[:, HT:HT + TT * NEXP].rearrange("p (t e) -> p t e", e=NEXP),
                                  each_tile(gate_b[:]), ALU.add))
            rstep(d.tensor_reduce(best[:], logit[:], AX.X, ALU.max))
            rstep(d.tensor_tensor(isbest[:], logit[:], each_expert(best[:]), ALU.is_equal))
            rstep(d.tensor_tensor(logit[:], isbest[:], each_tile(prio[:]), ALU.mult))
            rstep(d.tensor_reduce(best[:], logit[:], AX.X, ALU.max))
            d.tensor_tensor(onehot[:, 0:TT], logit[:], each_expert(best[:]), ALU.is_equal).then_inc(onehot_ok, 1)
            dve.wait_ge(onehot_ok, 1)
            dve.wait_ge(count_ps, 1)
            counts = lin_bank[0][:, 0, 0:(TT + 1) * NEXP].rearrange("p (t e) -> p t e", e=NEXP)
            rstep(d.tensor_scalar(ntile[:], counts[:, TT], 1.0 / P, (P - 1) / 2 / P, ALU.mult, ALU.add))
            rstep(d.tensor_scalar(ntile[:], ntile[:], ROUND, ROUND, ALU.add, ALU.subtract))
            rstep(d.tensor_tensor(prod[:], earlier[:], each_tile(ntile[:], NEXP), ALU.mult))
            rstep(d.tensor_reduce(first[:], prod[:], AX.X, ALU.add))
            rstep(d.scalar_tensor_tensor(place[:], each_tile(first[:]), float(P), counts[:, 0:TT], ALU.mult, ALU.add))
            rstep(d.tensor_tensor(place[:], place[:], onehot[:, 0:TT], ALU.mult))
            rstep(d.tensor_reduce(slot_f[:], place[:], AX.X, ALU.add))
            d.tensor_copy(slot[:], slot_f[:]).then_inc(slot_ok, 1)
            rstep(d.tensor_tensor(started[:], each_expert(tile_no[:], SLOT_TILES), each_tile(first[:], SLOT_TILES),
                                  ALU.is_ge))
            rstep(d.tensor_reduce(expert_f[:], started[:], AX.X, ALU.add))
            d.tensor_scalar(expert[:], expert_f[:], -1.0, None, ALU.add).then_inc(expert_ok, 1)

            def slots_T(j):
                dve.wait_ge(slotT_ps, j + 1)
                if j >= 3:
                    dve.wait_ge(up_ps, (j - 2) * HM)
                d.tensor_copy(xT[:, j % 3], slotT_bank[j % 2][0:EC, 0:2 * P].bitcast(F16).rearrange(
                    "p (s n) -> p s n", s=4)).then_inc(slotT_ok, 1)

            def finish(j):
                e = dve.value_load(expert[0:1, j:j + 1], min_val=0, max_val=NEXP - 1)
                d.tensor_tensor(hres[:, j % 2], xs[:, j, 0:E], b2[:, bass.ds(e, 1), :].rearrange("p e n -> p (e n)"),
                                ALU.add).then_inc(res_ok, 1)
                dve.wait_ge(res_ok, j + 1)
                dve.wait_ge(down_ps, j + 1)
                if j >= YB:
                    dve.wait_ge(stored[j % YB], 16 * (j // YB))
                d.scalar_tensor_tensor(yo[:, j % YB], down_bank[j % 2][:, 0:E], 1.0 / WSCALE, hres[:, j % 2],
                                       ALU.mult, ALU.add).then_inc(y_ok, 1)

            dve.wait_ge(expert_ok, 1)
            dve.wait_ge(b12_in, 32)
            slots_T(0)
            slots_T(1)
            for j in range(SLOT_TILES):
                dve.wait_ge(g_ok, (j + 1) * HM)
                if j >= 2:
                    dve.wait_ge(down_ps, j - 1)
                d.tensor_copy(gs[:, j % 2, 0], g[:, j % 2]).then_inc(ghi_ok, 1)
                dve.wait_ge(ghi_ok, j + 1)
                d.tensor_tensor(gs[:, j % 2, 1], g[:, j % 2], gs[:, j % 2, 0], ALU.subtract).then_inc(glo_ok, 1)
                if j + 2 < SLOT_TILES:
                    slots_T(j + 2)
                if j >= 1:
                    finish(j - 1)
            finish(SLOT_TILES - 1)

        @block.tensor
        def _(pe):
            mm = nc.tensor.matmul

            def embed(t):
                pe.wait_ge(patch_in[t], 16)
                if t >= 4:
                    pe.wait_ge(h_ok, t - 3)
                for kc in range(KE):
                    last = mm(emb_bank[t % 4][:, 0:E], patches[:, t, kc], proj_w[:, kc], start=kc == 0, stop=kc == KE - 1)
                last.then_inc(emb_ps, 1)

            def tokens_T(c):
                pe.wait_ge(xq_ok, c * CH // P + 3)
                if c >= 1:
                    pe.wait_ge(xqT_ok, c)
                out = score_bank[0:EC, :].bitcast(BF16)[:, 0:2 * 3 * P].rearrange("p (c n) -> p c n", c=2)
                for x in range(3):
                    t = c * CH // P + x
                    for h in range(2):
                        last = nc.tensor.transpose(out[:, h, x * P:(x + 1) * P], xq[:, t, h * EC:(h + 1) * EC], identb[:])
                last.then_inc(xqT_ps, 1)

            def ring_free(n):
                if n < 2:
                    return
                kind, m = ring[n - 2]
                pe.wait_ge({"lin": lin_int, "proj": h2_ok, "xnT": xnT_ok}[kind], m + 1)

            def linear(x):
                kind, c, n = x
                r = ring_no[("lin", lin_no[x])]
                bank = lin_bank[r % 2]
                ring_free(r)
                if n == 0:
                    pe.wait_ge(xqT_ok, c + 1)
                    pe.wait_ge(w_quant, {"q": 2, "k": 4, "v": 6}[kind])
                for half in range(2):
                    for kc in range(2):
                        if kind == "v":
                            p, w0 = c * PPC + n, 2 * INNER + half * INNER // 2
                            last = mm(bank[:, half, 0:INNER // 2], xqT[:, kc, 2 * p:2 * p + 2, :].rearrange("p i n -> p (i n)"),
                                      ww1q[:, kc, w0:w0 + INNER // 2], start=kc == 0, stop=kc == 1)
                        else:
                            m = 2 * n + half + (HB if kind == "k" else 0)
                            last = mm(bank[:, half, 0:CH], ww1q[:, kc, m * P:(m + 1) * P],
                                      xqT[:, kc, c * CI:(c + 1) * CI, 0:NTOK], start=kc == 0, stop=kc == 1)
                last.then_inc(lin_ps, 1)

            def scores(p):
                c, r = divmod(p, PPC)
                if r == 0:
                    pe.wait_ge(q_ok, c + 1)
                    pe.wait_ge(k_ok, 2 * c + 2)
                for m in range(HB):
                    for par in range(2):
                        i = 2 * r + par
                        last = mm(score_bank[64 * par:64 * par + NTOK, m * 2 * NTOK:(m + 1) * 2 * NTOK],
                                  q[:, c % 2, m, i * NTOK:(i + 1) * NTOK], k[:, c % 2, m, i].rearrange("p h n -> p (h n)"),
                                  start=True, stop=True)
                last.then_inc(s_ps, 1)

            def probs_T(p):
                pe.wait_ge(aq_ok, p + 1)
                if p >= 1:
                    pe.wait_ge(aT_ok, p)
                dst = probT_bank[:, 0:HT // 2].bitcast(BF16)
                for h in range(HEADS):
                    for par in range(2):
                        rows = slice(64 * par, 64 * par + NTOK)
                        last = nc.tensor.transpose(dst[rows, h * NTOK:(h + 1) * NTOK],
                                                   aq[rows, p % 2, h * NTOK:(h + 1) * NTOK], identb[rows, rows])
                last.then_inc(aT_ps, 1)

            def attend(p):
                pe.wait_ge(aT_ok, p + 1)
                pe.wait_ge(v_ok, p + 1)
                if p >= 1:
                    pe.wait_ge(o_int, p)
                for m in range(HB):
                    for hp in range(2):
                        for par in range(2):
                            rows = slice(64 * par, 64 * par + NTOK)
                            h = 2 * m + hp
                            last = mm(head_bank[64 * hp:64 * hp + 64, par, m * NTOK:(m + 1) * NTOK],
                                      v[rows, p % (2 * PPC), h * DH:(h + 1) * DH],
                                      aT[rows, p % 2, h * NTOK:(h + 1) * NTOK], start=True, stop=True)
                last.then_inc(o_ps, 1)

            def project(t):
                r = ring_no[("proj", t)]
                ring_free(r)
                pe.wait_ge(o_ok, -(-(t + 1) * P // (4 * NTOK)))
                pe.wait_ge(w_quant, len(WCH))
                for m in range(HB):
                    last = mm(lin_bank[r % 2][:, 0, 0:E], oT[:, m, t * P:(t + 1) * P], ww2q[:, m], start=m == 0,
                              stop=m == HB - 1)
                last.then_inc(pr_ps, 1)

            def norm_T(t):
                r = ring_no[("xnT", t)]
                ring_free(r)
                pe.wait_ge(xn_ok, t + 1)
                for c in range(2):
                    last = nc.tensor.transpose(lin_bank[r % 2][0:EC, 0, c * P:(c + 1) * P],
                                               xn[:, t % 2, c * EC:(c + 1) * EC], ident[:])
                last.then_inc(xnT_ps, 1)

            def gate(t):
                pe.wait_ge(xnT_ok, t + 1)
                pe.wait_ge(gate_in, 32)
                for c in range(2):
                    last = mm(score_bank[:, HT + t * NEXP:HT + (t + 1) * NEXP], xnT[:, t % 2, c], gate_w[:, c],
                              start=c == 0, stop=c == 1)
                last.then_inc(gate_ps, 1)

            pe.wait_ge(proj_in, 16)
            pe.wait_ge(psum_clear, 2)
            for t in range(5):
                embed(t)
            pe.wait_ge(ident_ok, 3)
            tokens_T(0)
            for t in range(5, 7):
                embed(t)
            tokens_T(1)
            for t in range(7, TT):
                embed(t)
            pe.wait_ge(h_ok, TT)
            for x in lin_groups(-1):
                linear(x)
            tokens_T(2)
            tokens_T(3)
            pe.wait_ge(xqT_ok, CHUNKS)
            scores(0)
            for i in range(STEPS):
                for x in lin_groups(i):
                    linear(x)
                if 0 <= i - 2 < PAIRS:
                    attend(i - 2)
                for t in tiles_at(i, 0):
                    project(t)
                for t in tiles_at(i, 3):
                    norm_T(t)
                if i < PAIRS:
                    pe.wait_ge(dif_ok, i + 1)
                for t in tiles_at(i, 4):
                    gate(t)
                if i + 1 < PAIRS:
                    scores(i + 1)
                if 0 <= i - 1 < PAIRS:
                    probs_T(i - 1)

            pe.wait_ge(onehot_ok, 1)
            pe.wait_ge(const_ok, NCONST)
            pe.wait_ge(xnT_ok, TT)
            count = lin_bank[0][:, 0, 0:(TT + 1) * NEXP]
            mm(count, before[:], onehot[:].rearrange("p t e -> p (t e)"), start=True, stop=False)
            for t in range(TT):
                last = mm(count[:, (t + 1) * NEXP:].rearrange("p (t e) -> p t e", e=NEXP), ones[:],
                          onehot[:, t:t + 1].to_broadcast([P, TT - t, NEXP]), start=False, stop=t == TT - 1)
            last.then_inc(count_ps, 1)

            def slots_T(j):
                pe.wait_ge(xs_in[j], 16)
                if j >= 2:
                    pe.wait_ge(slotT_ok, j - 1)
                out = slotT_bank[j % 2][0:EC, 0:2 * P].bitcast(F16).rearrange("p (s n) -> p s n", s=4)
                for s in range(4):
                    last = nc.tensor.transpose(out[:, s], xs16[:, j, 2 * E + s * EC:2 * E + (s + 1) * EC], identh[:])
                last.then_inc(slotT_ps, 1)

            PARTS = [(0, 0), (0, 1), (1, 0)]

            def up(j, e):
                pe.wait_ge(slotT_ok, j + 1)
                for m in range(HM):
                    n = j * HM + m
                    if n >= 4:
                        pe.wait_ge(g_ok, n - 3)
                    for x, (sw, sx) in enumerate(PARTS):
                        for c in range(2):
                            last = mm(up_bank[n % 4][:, 0:P], w1[:, bass.ds(e, 1), sw, c, m * P:(m + 1) * P].rearrange(
                                          "p e n -> p (e n)"), xT[:, j % 3, 2 * sx + c],
                                      start=x == 0 and c == 0, stop=x == 2 and c == 1)
                    last.then_inc(up_ps, 1)

            def down(j, e):
                pe.wait_ge(glo_ok, j + 1)
                if j >= 2:
                    pe.wait_ge(y_ok, j - 1)
                for x, (sg, sw) in enumerate(PARTS):
                    for m in range(HM):
                        last = mm(down_bank[j % 2][:, 0:E], gs[:, j % 2, sg, m],
                                  w2[:, bass.ds(e, 1), sw, m, :].rearrange("p e n -> p (e n)"),
                                  start=x == 0 and m == 0, stop=x == 2 and m == HM - 1)
                last.then_inc(down_ps, 1)

            pe.wait_ge(wlo_ok, len(SPLITS))
            pe.wait_ge(expert_ok, 1)
            slots_T(0)
            slots_T(1)
            e_before = None
            for j in range(SLOT_TILES):
                e = pe.value_load(expert[0:1, j:j + 1], min_val=0, max_val=NEXP - 1)
                up(j, e)
                if j + 2 < SLOT_TILES:
                    slots_T(j + 2)
                if j >= 1:
                    down(j - 1, e_before)
                e_before = e
            down(SLOT_TILES - 1, e_before)


_OUT = ((32, 36, 192), "float32")


def kernel(**inputs):
    import numpy as np
    import concourse.bacc as bacc
    from concourse.bass_utils import run_bass_kernel_spmd

    a = {k: np.asarray(x) for k, x in inputs.items()}
    imgs, cin, hh, ww = a["x"].shape
    ps = 16
    kdim = cin * ps * ps
    tok = imgs * (hh // ps) * (ww // ps)
    emb = a["L0_tok_proj_w"].shape[0]
    inner = a["L0_attn_ww2"].shape[1]
    nexp, _, hid = a["L0_ffn_W1"].shape
    x = a["x"].reshape(imgs, cin, hh // ps, ps, ww // ps, ps).transpose(1, 3, 5, 0, 2, 4)
    x = x.reshape(kdim // 128, 128, tok // 128, 128).transpose(1, 2, 0, 3)
    names = ("x1", "w1", "q", "k", "a", "v", "x2", "w2")
    quant = np.concatenate([a[f"L0_attn_s{n}"].reshape(1) for n in names] +
                           [a[f"L0_attn_z{n}"].reshape(1) for n in names])

    def rows(w, r):
        return w.reshape(w.shape[0] // r, r, w.shape[1]).transpose(1, 0, 2)

    arrays = {
        "patches": x,
        "proj_w": rows(a["L0_tok_proj_w"].T, 128),
        "proj_b": a["L0_tok_proj_b"],
        "quant": quant,
        "ww1": rows(a["L0_attn_ww1"].T, emb // 2),
        "ww2": rows(a["L0_attn_ww2"].T, 128),
        "bb2": a["L0_attn_bb2"],
        "gate_w": rows(a["L0_ffn_Wg"], emb // 2),
        "gate_b": a["L0_ffn_bg"],
        "w1": a["L0_ffn_W1"].reshape(nexp, 2, emb // 2, hid).transpose(2, 0, 1, 3),
        "b1": a["L0_ffn_b1"].reshape(nexp, hid // 128, 128).transpose(2, 0, 1),
        "w2": a["L0_ffn_W2"].reshape(nexp, hid // 128, 128, emb).transpose(2, 0, 1, 3),
        "b2": a["L0_ffn_b2"],
    }
    nc = bacc.Bacc("TRN2", target_bir_lowering=False, num_devices=1)
    args, sent = [], {}
    for name, arr in arrays.items():
        sent[f"in_{name}"] = np.ascontiguousarray(arr)
        args.append(nc.dram_tensor(f"in_{name}", arr.shape, mybir.dt.from_np(arr.dtype), kind="ExternalInput").ap())
    args.append(nc.dram_tensor("out_0", (tok, emb), F32, kind="ExternalOutput").ap())
    vit_kernel(nc, *args)
    r = run_bass_kernel_spmd(nc, [sent], core_ids=[0])
    return r.results[0]["out_0"].reshape(_OUT[0])
```

```python
from contextlib import ExitStack

import concourse.bass as bass
from concourse import mybir

F32 = mybir.dt.float32
BF16 = mybir.dt.bfloat16
F16 = mybir.dt.float16
I16 = mybir.dt.int16
I32 = mybir.dt.int32
U32 = mybir.dt.uint32
ALU = mybir.AluOpType
ACT = mybir.ActivationFunctionType
AX = mybir.AxisListType

P = 128
ROUND = 1.5 * 2.0 ** 23
QMAX = 15.0
EPS = 1e-5
WSCALE = 64.0
YB = 4
NCONST = 3 + 4 + 3 + 4 + 12
X1, W1Q, QQ, KQ, AQ, VQ, X2, W2Q = range(8)


def vit_kernel(nc, patches_d, proj_w_d, proj_b_d, quant_d, ww1_d, ww2_d, bb2_d,
               gate_w_d, gate_b_d, w1_d, b1_d, w2_d, b2_d, out_d):
    _, TT, KE, _ = patches_d.shape
    T = TT * P
    E = proj_w_d.shape[2]
    EC = E // 2
    NTOK = 36
    IMGS = T // NTOK
    PAIRS = IMGS // 2
    HEADS, DH = 12, 64
    INNER = HEADS * DH
    HB = INNER // P
    _, NEXP, HM = b1_d.shape
    HID = HM * P
    CH = 288
    CI = CH // NTOK
    CHUNKS = T // CH
    PPC = PAIRS // CHUNKS
    HT = HEADS * NTOK
    TRI = 3
    TR = TRI * NTOK
    TRIS = HEADS // TRI
    G3 = HEADS // (2 * TRI)
    SG = 2 * TRIS
    SLOT_TILES = (T + NEXP * (P - 1)) // P
    SLOTS = SLOT_TILES * P
    ROW = 2 * E + 4
    QG, VG = HB // 2, PPC

    with ExitStack() as ctx:
        def sb(name, shape, dt=F32):
            return ctx.enter_context(nc.sbuf_tensor(name, shape, dt))

        def sem(name):
            return ctx.enter_context(nc.semaphore(name))

        def psum(name, shape):
            return ctx.enter_context(nc.psum_tensor(name, shape, F32))

        lin_bank = [psum(f"lin_bank{i}", [P, 2, 512]) for i in range(2)]
        score_bank = psum("score_bank", [P, 512])
        probT_bank = psum("probT_bank", [P, 512])
        head_bank = psum("head_bank", [P, 2, 512])
        proj_bank = score_bank[:, SG * NTOK:SG * NTOK + E]
        xnT_bank = head_bank[:, 0, 256:512]
        gate_bank = head_bank[:, 1, 256:256 + TT * 4]
        emb_bank = [head_bank[:, 0], head_bank[:, 1], score_bank[:]]
        xqT_bank = probT_bank[0:EC].bitcast(BF16)[:, 0:2 * 3 * P].rearrange("p (c n) -> p c n", c=2)
        up_bank = [lin_bank[i // 2][:, i % 2] for i in range(4)]
        slotT_bank = [score_bank[:], probT_bank[:]]
        down_bank = [head_bank[:, 0], head_bank[:, 1]]

        patches = sb("patches", [P, TT, KE, P])
        proj_w = sb("proj_w", [P, KE, E])
        proj_b = sb("proj_b", [P, E])
        bb2 = sb("bb2", [P, E])
        quant = sb("quant", [P, 16])
        early = sb("early", [P, 6 * INNER])
        ww1 = early[0:EC].rearrange("p (c n) -> p c n", c=2)
        ww1q = sb("ww1q", [EC, 2, 3 * INNER], BF16)
        ww2 = sb("ww2", [P, HB, E])
        ww2q = sb("ww2q", [P, HB, E], BF16)
        inv = sb("inv", [P, 8])
        zr = sb("zr", [P, 8])
        lo = sb("lo", [P, 8])
        hi = sb("hi", [P, 8])
        fac = sb("fac", [P, 8])
        sxw, rq, rk, rv, cexp, ro, so, tmp = (fac[:, i:i + 1] for i in range(8))
        ident = sb("ident", [P, P])
        identb = sb("identb", [P, P], BF16)
        identh = sb("identh", [P, P], F16)
        before = sb("before", [P, P], BF16)
        ones = sb("ones", [P, P], BF16)
        row = sb("row", [P, TT, ROW])
        row16 = row[:].rearrange("p t n -> p (t n)").bitcast(F16).rearrange("p (t n) -> p t n", t=TT)
        blank = sb("blank", [P, ROW])
        stats = sb("stats", [P, 2, 6])
        mv = sb("mv", [P, TT, 2])
        veps = sb("veps", [P, TT])
        rstd = sb("rstd", [P, TT])
        rscale = sb("rscale", [P, TT])
        nhalf = sb("nhalf", [P, 1])
        xint = sb("xint", [P, 2, E], I16)
        xq = sb("xq", [P, TT, E], BF16)
        xqT = sb("xqT", [EC, 2, IMGS, DH], BF16)
        qkint = sb("qkint", [P, 2 * HB, CH], I16)
        QROW = G3 * CI * 4 * TR
        q = sb("q", [P, 2 * QROW + P - TR], BF16)
        q_slots = q[:, 0:2 * QROW].rearrange("p (b g i s n) -> p b g i s n", b=2, g=G3, i=CI, n=NTOK)
        k = sb("k", [P, 2, HB, CH], BF16)
        vint = sb("vint", [P, 2, INNER], I16)
        wint = vint
        VB = 2 * PPC - 1
        v = sb("v", [P, VB, INNER], BF16)
        mx = sb("mx", [P, 2, SG])
        den = sb("den", [P, 2, SG])
        dens = sb("dens", [P, 2, SG])
        rden = sb("rden", [P, 2, SG])
        dif = sb("dif", [P, 2, SG * NTOK])
        ex = sb("ex", [P, 2, SG * NTOK])
        aint = sb("aint", [P, 2, SG * NTOK], I16)
        aq = sb("aq", [P, 2, SG * NTOK], BF16)
        aT = sb("aT", [P, 2, HT], BF16)
        oint = sb("oint", [P, 2, HB, 4 * NTOK], I16)
        oT = sb("oT", [P, HB, T], BF16)
        xn = sb("xn", [P, 2, E])
        xnT = sb("xnT", [EC, 2, 2, P])
        gate_w = sb("gate_w", [EC, 2, NEXP])
        gate_b = sb("gate_b", [P, NEXP])
        prio = sb("prio", [P, NEXP])
        earlier = sb("earlier", [P, NEXP, NEXP])
        tile_no = sb("tile_no", [P, SLOT_TILES])
        logit = sb("logit", [P, TT, NEXP])
        isbest = sb("isbest", [P, TT, NEXP])
        best = sb("best", [P, TT])
        onehot = sb("onehot", [P, TT + 1, NEXP], BF16)
        ntile = sb("ntile", [P, NEXP])
        first = sb("first", [P, NEXP])
        prod = sb("prod", [P, NEXP, NEXP])
        place = sb("place", [P, TT, NEXP])
        slot = sb("slot", [P, TT], I32)
        started = sb("started", [P, SLOT_TILES, NEXP])
        expert = sb("expert", [P, SLOT_TILES], I32)
        expert_f = sb("expert_f", [P, SLOT_TILES])
        slot_f = sb("slot_f", [P, TT])
        b1 = sb("b1", [P, NEXP, HM])
        b2 = sb("b2", [P, NEXP, E])
        w1 = sb("w1", [EC, NEXP, 2, 2, HID], F16)
        w2 = early[:].bitcast(F16).rearrange("p (e m s n) -> p e m s n", e=NEXP, s=2, m=HM)
        warm = sb("warm", [1, 1])
        flat = patches[:].rearrange("p t k n -> p (t k n)")
        w1f = flat[0:EC, 0:NEXP * 2 * HID].rearrange("p (e c n) -> p e c n", e=NEXP, c=2)
        w2f = flat[:, 0:NEXP * 2 * HID].rearrange("p (e n) -> p e n", e=NEXP)[:, :, 0:HM * E].rearrange(
            "p e (m n) -> p e m n", m=HM)
        nx = SLOT_TILES * ROW
        xs = flat[:, 0:nx].rearrange("p (j n) -> p j n", n=ROW)
        xs16 = flat[:, 0:nx].bitcast(F16).rearrange("p (j n) -> p j n", n=2 * ROW)
        g = flat[:, nx:nx + 2 * HID].rearrange("p (b m n) -> p b m n", b=2, m=HM)
        late = q[:].bitcast(F32)
        gs = late[:, 0:2 * HID].bitcast(F16).rearrange("p (b s m n) -> p b s m n", b=2, s=2, m=HM)
        x0 = 2 * HID
        xT = late[0:EC, x0:x0 + 3 * 2 * P].bitcast(F16).rearrange("p (b s n) -> p b s n", b=3, s=4)
        y0 = x0 + 3 * 2 * P
        yo = late[:, y0:y0 + YB * E].rearrange("p (b n) -> p b n", b=YB)
        hres = late[:, y0 + YB * E:y0 + (YB + 2) * E].rearrange("p (b n) -> p b n", b=2)
        slots_d = nc.dram_tensor("slots", (SLOTS, ROW), F32).ap()

        (quant_in, proj_in, bias_in, bb2_in, ww1_in, ww2_in, gate_in, w1_in, b12_in, blank_out,
         scattered) = map(sem, (
             "quant_in", "proj_in", "bias_in", "bb2_in", "ww1_in", "ww2_in", "gate_in", "w1_in", "b12_in",
             "blank_out", "scattered"))
        stored = [sem(f"stored{b}") for b in range(YB)]
        w2_in = [sem(f"w2_in{e}") for e in range(NEXP)]
        patch_in = [sem(f"patch_in{t}") for t in range(TT)]
        xs_in = [sem(f"xs_in{j}") for j in range(SLOT_TILES)]
        pool_step, ident_ok, pad_ok, qpad_ok, blank_ok, const_ok, setup, scales_ok, psum_clear = map(sem, (
            "pool_step", "ident_ok", "pad_ok", "qpad_ok", "blank_ok", "const_ok", "setup", "scales_ok", "psum_clear"))
        w_int, w_quant, emb_ps, h_ok, stat_ok, aggr_ok, var_ok, rstd_ok, rscale_ok, norm_ok, xq_ok = map(sem, (
            "w_int", "w_quant", "emb_ps", "h_ok", "stat_ok", "aggr_ok", "var_ok", "rstd_ok", "rscale_ok",
            "norm_ok", "xq_ok"))
        hb_ok, xqT_ps, xqT_ok = map(sem, ("hb_ok", "xqT_ps", "xqT_ok"))
        lin_ps, lin_int, q_ok, k_ok, v_ok = map(sem, ("lin_ps", "lin_int", "q_ok", "k_ok", "v_ok"))
        s_ps, mx_ok, dif_ok, ex_ok, den_ok, dens_ok, rden_ok, aint_ok, aq_ok = map(sem, (
            "s_ps", "mx_ok", "dif_ok", "ex_ok", "den_ok", "dens_ok", "rden_ok", "aint_ok", "aq_ok"))
        aT_ps, aT_ok, o_ps, o_int, o_ok = map(sem, ("aT_ps", "aT_ok", "o_ps", "o_int", "o_ok"))
        pr_ps, h2_ok, xn_ok, xhi_ok, xlo_ok, xnT_ps, xnT_ok, gate_ps = map(sem, (
            "pr_ps", "h2_ok", "xn_ok", "xhi_ok", "xlo_ok", "xnT_ps", "xnT_ok", "gate_ps"))
        whi_ok, wlo_ok, route, onehot_ok, count_ps, slot_ok, expert_ok = map(sem, (
            "whi_ok", "wlo_ok", "route", "onehot_ok", "count_ps", "slot_ok", "expert_ok"))
        slotT_ps, slotT_ok, up_ps, g_ok, ghi_ok, glo_ok, down_ps, res_ok, y_ok = map(sem, (
            "slotT_ps", "slotT_ok", "up_ps", "g_ok", "ghi_ok", "glo_ok", "down_ps", "res_ok", "y_ok"))

        STEPS = PAIRS + 8

        def lin_groups(i):
            if i == -1:
                return [("q", 0, n) for n in range(QG)] + [("k", 0, n) for n in range(QG)]
            out = []
            c, r = divmod(i, PPC)
            if i < 2:
                out += [("v", 0, n) for n in range(i * VG // 2, (i + 1) * VG // 2)]
            if c + 1 < CHUNKS:
                if r == 0:
                    out += [("q", c + 1, n) for n in range(QG)]
                if r == 1:
                    out += [("k", c + 1, n) for n in range(QG)]
                if r >= 2:
                    out += [("v", c + 1, n) for n in range((r - 2) * VG // 2, (r - 1) * VG // 2)]
            return out

        def tiles_at(i, delay):
            return [t for t in range(TT) if i - delay == 4 + min(2 * t, t + TT - 2)]

        lin_no, lin_order = {}, []
        for i in range(-1, STEPS):
            for x in lin_groups(i):
                lin_no[x] = len(lin_order)
                lin_order.append(x)

        SPLITS = [(1, e, c) for e in range(NEXP) for c in range(2)] + [(2, e, c) for e in range(NEXP) for c in range(2)]

        def split_views(n):
            which, e, c = SPLITS[n]
            if which == 1:
                return w1f[:, e, c], w1[:, e, 0, c], w1[:, e, 1, c]
            ms = slice(c * HM // 2, (c + 1) * HM // 2)
            return w2f[:, e, ms], w2[:, e, ms, 0], w2[:, e, ms, 1]

        WCH = [(s, c) for s in range(3) for c in range(2)] + [(3, c) for c in range(2)]

        def weight_views(n):
            s, c = WCH[n]
            if s < 3:
                cols = slice(s * INNER, (s + 1) * INNER)
                return W1Q, ww1[:, c, cols], wint[0:EC, n % 2], ww1q[:, c, cols]
            ms = slice(c * HB // 2, (c + 1) * HB // 2)
            return W2Q, ww2[:, ms], wint[:, n % 2, 0:HB // 2 * E].rearrange("p (m n) -> p m n", n=E), ww2q[:, ms]

        def groups(x):
            return x.rearrange("p (h n) -> p h n", n=NTOK)

        block = ctx.enter_context(nc.Block())

        @block.sync
        def _(sp):
            sp.dma_start(quant[:], quant_d.partition_broadcast(P)).then_inc(quant_in, 16)
            sp.dma_start(proj_w[:], proj_w_d).then_inc(proj_in, 16)
            for t in range(TT):
                sp.dma_start(patches[:, t], patches_d[:, t]).then_inc(patch_in[t], 16)
                if t == 0:
                    sp.dma_start(proj_b[:], proj_b_d.partition_broadcast(P)).then_inc(bias_in, 16)
                    sp.dma_start(bb2[:], bb2_d.partition_broadcast(P)).then_inc(bb2_in, 16)
                if t == 2:
                    sp.dma_start(ww1, ww1_d).then_inc(ww1_in, 16)
            sp.dma_start(ww2[:], ww2_d).then_inc(ww2_in, 16)
            sp.dma_start(gate_w[:], gate_w_d).then_inc(gate_in, 16)
            sp.dma_start(gate_b[:], gate_b_d.partition_broadcast(P)).then_inc(gate_in, 16)
            sp.wait_ge(emb_ps, TT)
            sp.dma_start(w1f, w1_d).then_inc(w1_in, 16)
            sp.dma_start(b1[:], b1_d).then_inc(b12_in, 16)
            sp.dma_start(b2[:], b2_d.rearrange("e n -> (e n)").partition_broadcast(P)).then_inc(b12_in, 16)
            sp.wait_ge(blank_ok, 2)
            for j in range(SLOT_TILES):
                sp.dma_start(slots_d[j * P:(j + 1) * P, :], blank[:]).then_inc(blank_out, 16)
            for e in range(NEXP):
                sp.wait_ge(wlo_ok, 2 * e + 2)
                sp.dma_start(w2f[:, e], w2_d[:, e]).then_inc(w2_in[e], 16)
            sp.wait_ge(wlo_ok, len(SPLITS))
            sp.wait_ge(scattered, 16 * TT)
            for j in range(SLOT_TILES):
                sp.dma_start(xs[:, j], slots_d[j * P:(j + 1) * P, :]).then_inc(xs_in[j], 16)

        @block.gpsimd
        def _(pool):
            gp = nc.gpsimd
            steps = [0]

            def step(ins):
                steps[0] += 1
                ins.then_inc(pool_step, 1)
                pool.wait_ge(pool_step, steps[0])

            step(gp.memset(ident[:], 0.0))
            step(gp.affine_select(out=ident[:], in_=ident[:], compare_op=ALU.not_equal, fill=1.0, base=0,
                                  pattern=[[-1, P]], channel_multiplier=1))
            gp.tensor_copy(identb[:], ident[:]).then_inc(ident_ok, 1)
            gp.tensor_copy(identh[:], ident[:]).then_inc(ident_ok, 1)
            gp.memset(nhalf[:], -0.5).then_inc(ident_ok, 1)
            gp.memset(xqT[:], 0.0).then_inc(pad_ok, 1)
            gp.memset(q[:].bitcast(U32), 0).then_inc(qpad_ok, 1)
            pool.wait_ge(ident_ok, 3)
            for t in range(TT):
                pool.wait_ge(var_ok, t + 1)
                gp.tensor_tensor(rstd[:, t:t + 1], veps[:, t:t + 1], nhalf[:], ALU.pow).then_inc(rstd_ok, 1)
            pool.wait_ge(bb2_in, 16)
            for t in range(TT):
                pool.wait_ge(norm_ok, t + 1)
                gp.tensor_tensor(row[:, t, 0:E], row[:, t, 0:E], bb2[:], ALU.add).then_inc(hb_ok, 1)
            step(gp.memset(blank[:, 0:2 * E], 0.0))
            gp.iota(blank[:, 2 * E:ROW].bitcast(I32), pattern=[[0, 4]], base=T, channel_multiplier=1).then_inc(blank_ok, 1)
            gp.iota(row[:, :, 2 * E:ROW].bitcast(I32), pattern=[[P, TT], [0, 4]], base=0,
                    channel_multiplier=1).then_inc(blank_ok, 1)
            step(gp.memset(before[:], 1.0))
            gp.affine_select(out=before[:], in_=before[:], compare_op=ALU.is_gt, fill=0.0, base=0,
                             pattern=[[1, P]], channel_multiplier=-1).then_inc(const_ok, 1)
            gp.memset(ones[:], 1.0).then_inc(const_ok, 1)
            gp.memset(onehot[:, TT], 0.0).then_inc(const_ok, 1)
            for e in range(NEXP):
                gp.memset(prio[:, e:e + 1], float(NEXP - e)).then_inc(const_ok, 1)
                if e:
                    gp.memset(earlier[:, e, 0:e], 1.0).then_inc(const_ok, 1)
                gp.memset(earlier[:, e, e:], 0.0).then_inc(const_ok, 1)
            for j in range(SLOT_TILES):
                gp.memset(tile_no[:, j:j + 1], float(j)).then_inc(const_ok, 1)
            for t in range(TT):
                pool.wait_ge(var_ok, TT + t + 1)
                gp.tensor_tensor(rstd[:, t:t + 1], veps[:, t:t + 1], nhalf[:], ALU.pow).then_inc(rstd_ok, 1)
            pool.wait_ge(blank_out, 16 * SLOT_TILES)
            pool.wait_ge(xlo_ok, TT)
            pool.wait_ge(xhi_ok, TT)
            pool.wait_ge(slot_ok, 1)
            for t in range(TT):
                gp.indirect_dma_start(out=slots_d, out_offset=bass.IndirectOffsetOnAxis(ap=slot[:, t:t + 1], axis=0),
                                      in_=row[:, t, :], in_offset=None,
                                      bounds_check=SLOTS - 1, oob_is_err=False).then_inc(scattered, 16)
            for j in range(SLOT_TILES):
                pool.wait_ge(y_ok, j + 1)
                gp.indirect_dma_start(out=out_d, out_offset=bass.IndirectOffsetOnAxis(
                                          ap=xs[:, j, 2 * E:2 * E + 1].bitcast(I32), axis=0),
                                      in_=yo[:, j % YB, :], in_offset=None,
                                      bounds_check=T - 1, oob_is_err=False).then_inc(stored[j % YB], 16)
            for b in range(YB):
                pool.wait_ge(stored[b], 16 * (SLOT_TILES // YB))

        @block.scalar
        def _(act):
            a = nc.scalar

            def weights(n):
                s, w, wi, _ = weight_views(n)
                if n >= 2:
                    act.wait_ge(w_quant, n - 1)
                a.activation(wi, w, ACT.Copy, scale=inv[0:w.shape[0], s:s + 1]).then_inc(w_int, 1)

            def tokens_T(c):
                act.wait_ge(xqT_ps, c + 1)
                off = c * CH % P
                a.copy(xqT[:, :, c * CI:(c + 1) * CI, 0:NTOK],
                       xqT_bank[:, :, off:off + CH].rearrange("p c (i n) -> p c i n", n=NTOK)).then_inc(xqT_ok, 1)

            def linear(x):
                kind, c, n = x
                j = lin_no[x]
                bank = lin_bank[j % 2]
                act.wait_ge(lin_ps, j + 1)
                if kind == "v":
                    p = c * PPC + n
                    if p == 0:
                        act.wait_ge(w_quant, len(WCH))
                    if p >= 2:
                        act.wait_ge(v_ok, p - 1)
                    a.activation(vint[:, p % 2].rearrange("p (s n) -> p s n", s=2), bank[:, :, 0:INNER // 2],
                                 ACT.Copy, scale=rv).then_inc(lin_int, 1)
                    return
                m = 2 * n
                if kind == "k":
                    m += HB
                if c >= 1 and n == 0:
                    act.wait_ge(q_ok if kind == "q" else k_ok, 4 * c if kind == "q" else c)
                a.activation(qkint[:, m:m + 2], bank[:, :, 0:CH], ACT.Copy,
                             scale=rq if kind == "q" else rk).then_inc(lin_int, 1)

            act.wait_ge(scales_ok, 1)
            act.wait_ge(ww1_in, 16)
            act.wait_ge(pad_ok, 1)
            for n in range(4):
                weights(n)
            tokens_T(0)
            weights(4)
            for x in lin_groups(-1)[:QG]:
                linear(x)
            weights(5)
            for x in lin_groups(-1)[QG:]:
                linear(x)
            tokens_T(1)
            act.wait_ge(ww2_in, 16)
            weights(6)
            weights(7)
            for i in range(STEPS):
                if 1 <= i <= len(SPLITS):
                    if i == 1:
                        act.wait_ge(w1_in, 16)
                    which, e, _ = SPLITS[i - 1]
                    if which == 2:
                        act.wait_ge(w2_in[e], 16)
                    w, whi, _ = split_views(i - 1)
                    a.activation(whi, w, ACT.Copy, scale=WSCALE).then_inc(whi_ok, 1)
                if i < PAIRS:
                    b = i % 2
                    act.wait_ge(dif_ok, i + 1)
                    if i >= 2:
                        act.wait_ge(aint_ok, i - 1)
                    a.activation(ex[0:TR, b], dif[0:TR, b], ACT.Exp, scale=cexp[0:TR]).then_inc(ex_ok, 1)
                for x in lin_groups(i)[:1]:
                    linear(x)
                if 2 <= i < CHUNKS:
                    tokens_T(i)
                p = i - 2
                if 0 <= p < PAIRS:
                    act.wait_ge(o_ps, p + 1)
                    if p >= 4 and p % 2 == 0:
                        act.wait_ge(o_ok, p // 2 - 1)
                    dst = oint[:, p // 2 % 2, :, (p % 2) * 2 * NTOK:(p % 2 + 1) * 2 * NTOK]
                    a.activation(dst.rearrange("p m (r n) -> p r m n", r=2),
                                 head_bank[:, :, 0:HB * NTOK].rearrange("p r (m n) -> p r m n", m=HB),
                                 ACT.Copy, scale=ro).then_inc(o_int, 1)
                for x in lin_groups(i)[1:]:
                    linear(x)
                for t in tiles_at(i, 2):
                    act.wait_ge(xn_ok, t + 1)
                    a.copy(row16[:, t, 2 * E:3 * E], xn[:, t % 2]).then_inc(xhi_ok, 1)
                p = i - 1
                if 0 <= p < PAIRS:
                    act.wait_ge(aT_ps, p + 1)
                    if p >= 2:
                        act.wait_ge(o_ps, p - 1)
                    a.copy(aT[:, p % 2], probT_bank[:, 0:HT // 2].bitcast(BF16)).then_inc(aT_ok, 1)
                for t in tiles_at(i, 3):
                    act.wait_ge(xnT_ps, t + 1)
                    if t >= 2:
                        act.wait_ge(gate_ps, t - 1)
                    a.copy(xnT[:, t % 2], xnT_bank[0:EC].rearrange(
                        "p (c n) -> p c n", c=2)).then_inc(xnT_ok, 1)
            act.wait_ge(const_ok, 1)
            a.activation(warm[:], nhalf[0:1], ACT.Gelu)
            act.wait_ge(b12_in, 32)
            act.wait_ge(expert_ok, 1)
            experts = [act.value_load(expert[0:1, j:j + 1], min_val=0, max_val=NEXP - 1) for j in range(SLOT_TILES)]
            for j, e in enumerate(experts):
                for m in range(HM):
                    n = j * HM + m
                    act.wait_ge(up_ps, n + 1)
                    if j >= 2 and m == 0:
                        act.wait_ge(glo_ok, j - 1)
                    a.activation(g[:, j % 2, m], up_bank[n % 4][:, 0:P], ACT.Gelu, scale=1.0 / WSCALE,
                                 bias=b1[:, bass.ds(e, 1), m]).then_inc(g_ok, 1)

        @block.vector
        def _(dve):
            d = nc.vector
            steps = [0]

            def step(ins):
                steps[0] += 1
                ins.then_inc(setup, 1)
                dve.wait_ge(setup, steps[0])

            def mul(out, x, y):
                step(d.tensor_tensor(out, x, y, ALU.mult))

            d.memset(probT_bank[:], 0.0).then_inc(psum_clear, 1)
            dve.wait_ge(quant_in, 16)
            scl, zero = quant[:, 0:8], quant[:, 8:16]
            step(d.reciprocal(inv[:], scl))
            step(d.tensor_scalar(zr[:], zero, ROUND, ROUND, ALU.add, ALU.subtract))
            step(d.tensor_scalar(lo[:], zr[:], -1.0, None, ALU.mult))
            step(d.tensor_scalar(hi[:], zr[:], -1.0, QMAX, ALU.mult, ALU.add))
            mul(sxw, scl[:, X1:X1 + 1], scl[:, W1Q:W1Q + 1])
            mul(rq, sxw, inv[:, QQ:QQ + 1])
            mul(rk, sxw, inv[:, KQ:KQ + 1])
            mul(rv, sxw, inv[:, VQ:VQ + 1])
            mul(tmp, scl[:, QQ:QQ + 1], scl[:, KQ:KQ + 1])
            step(d.tensor_scalar(cexp, tmp, DH ** -0.5, None, ALU.mult))
            mul(tmp, scl[:, AQ:AQ + 1], scl[:, VQ:VQ + 1])
            mul(ro, tmp, inv[:, X2:X2 + 1])
            d.tensor_tensor(so, scl[:, X2:X2 + 1], scl[:, W2Q:W2Q + 1], ALU.mult).then_inc(scales_ok, 1)
            dve.wait_ge(scales_ok, 1)

            def clip(out, x, s, n=P, base=0):
                return d.tensor_scalar(out, x, lo[base:base + n, s:s + 1], hi[base:base + n, s:s + 1],
                                       ALU.max, ALU.min)

            def weights(n):
                s, w, wi, wq = weight_views(n)
                dve.wait_ge(w_int, n + 1)
                clip(wq, wi, s, w.shape[0]).then_inc(w_quant, 1)

            def moments(t, n):
                d.bn_stats(stats[:, n % 2], row[:, t, 0:E]).then_inc(stat_ok, 1)

            def variance(t, n):
                dve.wait_ge(stat_ok, n + 1)
                d.bn_aggr(mv[:, t], stats[:, n % 2]).then_inc(aggr_ok, 1)

            def guard(t, n):
                dve.wait_ge(aggr_ok, n + 1)
                d.tensor_scalar(veps[:, t:t + 1], mv[:, t, 1:2], EPS, None, ALU.add).then_inc(var_ok, 1)

            def token_scale(t):
                dve.wait_ge(rstd_ok, t + 1)
                d.tensor_tensor(rscale[:, t:t + 1], rstd[:, t:t + 1], inv[:, X1:X1 + 1], ALU.mult).then_inc(rscale_ok, 1)

            def round_tokens(t):
                dve.wait_ge(rscale_ok, t + 1)
                d.tensor_scalar(xint[:, t % 2], row[:, t, 0:E], mv[:, t, 0:1], rscale[:, t:t + 1],
                                ALU.subtract, ALU.mult).then_inc(norm_ok, 1)

            def clip_tokens(t):
                dve.wait_ge(norm_ok, t + 1)
                clip(xq[:, t], xint[:, t % 2], X1).then_inc(xq_ok, 1)

            def linear(x):
                kind, c, n = x
                dve.wait_ge(lin_int, lin_no[x] + 1)
                if kind == "q":
                    if c >= 2:
                        dve.wait_ge(s_ps, (c - 1) * PPC)
                    if c == 0:
                        dve.wait_ge(qpad_ok, 1)
                    for g in range(G3):
                        for upper in range(2):
                            rows = slice(DH * upper, DH * upper + DH)
                            clip(q_slots[rows, c % 2, g, :, upper:upper + 11:5], qkint[rows, TRI * g:TRI * (g + 1)].rearrange(
                                     "p t (i n) -> p i t n", n=NTOK), QQ, DH, DH * upper).then_inc(q_ok, 1)
                elif kind == "k":
                    if c >= 2:
                        dve.wait_ge(s_ps, (c - 1) * PPC)
                    clip(k[:, c % 2], qkint[:, HB:2 * HB], KQ).then_inc(k_ok, 1)
                else:
                    p = c * PPC + n
                    if p >= VB:
                        dve.wait_ge(o_ps, p - VB + 1)
                    clip(v[:, p % VB], vint[:, p % 2], VQ).then_inc(v_ok, 1)

            def clips_of(i):
                return [x for x in lin_groups(i) if x[0] == "v" or x[2] == QG - 1]

            for t in range(TT):
                dve.wait_ge(emb_ps, t + 1)
                if t == 0:
                    dve.wait_ge(bias_in, 16)
                d.tensor_tensor(row[:, t, 0:E], emb_bank[t % 3][:, 0:E], proj_b[:], ALU.add).then_inc(h_ok, 1)
                if t >= 1:
                    token_scale(t - 1)
                dve.wait_ge(h_ok, t + 1)
                moments(t, t)
                if t >= 1:
                    round_tokens(t - 1)
                variance(t, t)
                if t >= 1:
                    clip_tokens(t - 1)
                guard(t, t)
                if t >= 2:
                    weights(t - 2)
                if t == 6:
                    linear(lin_groups(-1)[QG - 1])
                if t == 7:
                    linear(lin_groups(-1)[2 * QG - 1])
            token_scale(TT - 1)
            round_tokens(TT - 1)
            clip_tokens(TT - 1)
            for n in range(TT - 2, len(WCH)):
                weights(n)

            for i in range(STEPS):
                new, old = i < PAIRS, 0 <= i - 1 < PAIRS
                b, p = i % 2, i - 1
                ob = p % 2
                for t in tiles_at(i, 1):
                    dve.wait_ge(pr_ps, t + 1)
                if new:
                    dve.wait_ge(s_ps, i + 1)
                    d.tensor_reduce(mx[0:TR, b], groups(score_bank[0:TR, 0:SG * NTOK]), AX.X, ALU.max).then_inc(mx_ok, 1)
                if old:
                    dve.wait_ge(ex_ok, p + 1)
                    d.tensor_reduce(den[0:TR, ob], groups(ex[0:TR, ob]), AX.X, ALU.add).then_inc(den_ok, 1)
                if new:
                    dve.wait_ge(mx_ok, i + 1)
                    if i >= 2:
                        dve.wait_ge(ex_ok, i - 1)
                    d.tensor_tensor(groups(dif[0:TR, b]), groups(score_bank[0:TR, 0:SG * NTOK]),
                                    mx[0:TR, b].unsqueeze(2).to_broadcast([TR, SG, NTOK]),
                                    ALU.subtract).then_inc(dif_ok, 1)
                for t in tiles_at(i, 1):
                    dve.wait_ge(hb_ok, t + 1)
                    d.scalar_tensor_tensor(row[:, t, 0:E], proj_bank, so, row[:, t, 0:E],
                                           ALU.mult, ALU.add).then_inc(h2_ok, 1)
                n = i - 4
                if n >= 0 and n % 2 == 0 and n // 2 < PAIRS // 2:
                    n //= 2
                    dve.wait_ge(o_int, 2 * n + 2)
                    clip(oT[:, :, n * 4 * NTOK:(n + 1) * 4 * NTOK], oint[:, n % 2], X2).then_inc(o_ok, 1)
                if old:
                    dve.wait_ge(den_ok, p + 1)
                    d.tensor_scalar(dens[0:TR, ob], den[0:TR, ob], scl[0:TR, AQ:AQ + 1], None,
                                    ALU.mult).then_inc(dens_ok, 1)
                clipped = clips_of(i - 1) if i else []
                values = [x for x in clipped if x[0] == "v"]
                for x in values[:1]:
                    linear(x)
                if old:
                    dve.wait_ge(dens_ok, p + 1)
                    d.reciprocal(rden[0:TR, ob], dens[0:TR, ob]).then_inc(rden_ok, 1)
                if old:
                    dve.wait_ge(rden_ok, p + 1)
                    d.tensor_tensor(groups(aint[0:TR, ob]), groups(ex[0:TR, ob]),
                                    rden[0:TR, ob].unsqueeze(2).to_broadcast([TR, SG, NTOK]),
                                    ALU.mult).then_inc(aint_ok, 1)
                for x in values[1:]:
                    linear(x)
                if old:
                    dve.wait_ge(aint_ok, p + 1)
                    if p >= 2:
                        dve.wait_ge(aT_ps, p - 1)
                    clip(aq[0:TR, ob], aint[0:TR, ob], AQ, TR).then_inc(aq_ok, 1)
                for t in tiles_at(i, 1):
                    dve.wait_ge(h2_ok, t + 1)
                    moments(t, TT + t)
                for t in tiles_at(i, 3):
                    dve.wait_ge(xhi_ok, t + 1)
                    d.tensor_tensor(row16[:, t, 3 * E:4 * E], xn[:, t % 2], row16[:, t, 2 * E:3 * E],
                                    ALU.subtract).then_inc(xlo_ok, 1)
                for t in tiles_at(i, 1):
                    variance(t, TT + t)
                for x in clipped:
                    if x[0] != "v":
                        linear(x)
                for t in tiles_at(i, 1):
                    guard(t, TT + t)
                for t in tiles_at(i, 2):
                    dve.wait_ge(rstd_ok, TT + t + 1)
                    if t >= 2:
                        dve.wait_ge(xnT_ps, t - 1)
                        dve.wait_ge(xlo_ok, t - 1)
                    d.tensor_scalar(xn[:, t % 2], row[:, t, 0:E], mv[:, t, 0:1], rstd[:, t:t + 1],
                                    ALU.subtract, ALU.mult).then_inc(xn_ok, 1)
                if 2 <= i < 2 + len(SPLITS):
                    w, whi, wlo = split_views(i - 2)
                    dve.wait_ge(whi_ok, i - 1)
                    d.scalar_tensor_tensor(wlo, w, WSCALE, whi, ALU.mult, ALU.subtract).then_inc(wlo_ok, 1)

            routed = [0]

            def rstep(ins):
                routed[0] += 1
                ins.then_inc(route, 1)
                dve.wait_ge(route, routed[0])

            def each_expert(x, n=TT):
                return x.unsqueeze(2).to_broadcast([P, n, NEXP])

            def each_tile(x, n=TT):
                return x.unsqueeze(1).to_broadcast([P, n, NEXP])

            dve.wait_ge(gate_in, 32)
            dve.wait_ge(const_ok, NCONST)
            dve.wait_ge(gate_ps, TT)
            rstep(d.tensor_tensor(logit[:], gate_bank.rearrange("p (t e) -> p t e", e=NEXP),
                                  each_tile(gate_b[:]), ALU.add))
            rstep(d.tensor_reduce(best[:], logit[:], AX.X, ALU.max))
            rstep(d.tensor_tensor(isbest[:], logit[:], each_expert(best[:]), ALU.is_equal))
            rstep(d.tensor_tensor(logit[:], isbest[:], each_tile(prio[:]), ALU.mult))
            rstep(d.tensor_reduce(best[:], logit[:], AX.X, ALU.max))
            d.tensor_tensor(onehot[:, 0:TT], logit[:], each_expert(best[:]), ALU.is_equal).then_inc(onehot_ok, 1)
            dve.wait_ge(onehot_ok, 1)
            dve.wait_ge(count_ps, 1)
            counts = lin_bank[0][:, 0, 0:(TT + 1) * NEXP].rearrange("p (t e) -> p t e", e=NEXP)
            rstep(d.tensor_scalar(ntile[:], counts[:, TT], 1.0 / P, (P - 1) / 2 / P, ALU.mult, ALU.add))
            rstep(d.tensor_scalar(ntile[:], ntile[:], ROUND, ROUND, ALU.add, ALU.subtract))
            rstep(d.tensor_tensor(prod[:], earlier[:], each_tile(ntile[:], NEXP), ALU.mult))
            rstep(d.tensor_reduce(first[:], prod[:], AX.X, ALU.add))
            rstep(d.scalar_tensor_tensor(place[:], each_tile(first[:]), float(P), counts[:, 0:TT], ALU.mult, ALU.add))
            rstep(d.tensor_tensor(place[:], place[:], onehot[:, 0:TT], ALU.mult))
            rstep(d.tensor_reduce(slot_f[:], place[:], AX.X, ALU.add))
            d.tensor_copy(slot[:], slot_f[:]).then_inc(slot_ok, 1)
            rstep(d.tensor_tensor(started[:], each_expert(tile_no[:], SLOT_TILES), each_tile(first[:], SLOT_TILES),
                                  ALU.is_ge))
            rstep(d.tensor_reduce(expert_f[:], started[:], AX.X, ALU.add))
            d.tensor_scalar(expert[:], expert_f[:], -1.0, None, ALU.add).then_inc(expert_ok, 1)

            def slots_T(j):
                dve.wait_ge(slotT_ps, j + 1)
                if j >= 3:
                    dve.wait_ge(up_ps, (j - 2) * HM)
                d.tensor_copy(xT[:, j % 3], slotT_bank[j % 2][0:EC, 0:2 * P].bitcast(F16).rearrange(
                    "p (s n) -> p s n", s=4)).then_inc(slotT_ok, 1)

            def finish(j):
                e = experts[j]
                d.tensor_tensor(hres[:, j % 2], xs[:, j, 0:E], b2[:, bass.ds(e, 1), :].rearrange("p e n -> p (e n)"),
                                ALU.add).then_inc(res_ok, 1)
                dve.wait_ge(res_ok, 2 * j + 1)
                dve.wait_ge(down_ps, j + 1)
                d.scalar_tensor_tensor(hres[:, j % 2], down_bank[j % 2][:, E:2 * E], 1.0 / WSCALE, hres[:, j % 2],
                                       ALU.mult, ALU.add).then_inc(res_ok, 1)
                dve.wait_ge(res_ok, 2 * j + 2)
                if j >= YB:
                    dve.wait_ge(stored[j % YB], 16 * (j // YB))
                d.scalar_tensor_tensor(yo[:, j % YB], down_bank[j % 2][:, 0:E], 1.0 / WSCALE, hres[:, j % 2],
                                       ALU.mult, ALU.add).then_inc(y_ok, 1)

            dve.wait_ge(expert_ok, 1)
            experts = [dve.value_load(expert[0:1, j:j + 1], min_val=0, max_val=NEXP - 1) for j in range(SLOT_TILES)]
            dve.wait_ge(b12_in, 32)
            slots_T(0)
            slots_T(1)
            for j in range(SLOT_TILES):
                dve.wait_ge(g_ok, (j + 1) * HM)
                if j >= 2:
                    dve.wait_ge(down_ps, j - 1)
                d.tensor_copy(gs[:, j % 2, 0], g[:, j % 2]).then_inc(ghi_ok, 1)
                dve.wait_ge(ghi_ok, j + 1)
                d.tensor_tensor(gs[:, j % 2, 1], g[:, j % 2], gs[:, j % 2, 0], ALU.subtract).then_inc(glo_ok, 1)
                if j + 2 < SLOT_TILES:
                    slots_T(j + 2)
                if j >= 1:
                    finish(j - 1)
            finish(SLOT_TILES - 1)

        @block.tensor
        def _(pe):
            mm = nc.tensor.matmul

            def embed(t):
                pe.wait_ge(patch_in[t], 16)
                if t >= 3:
                    pe.wait_ge(h_ok, t - 2)
                for kc in range(KE):
                    last = mm(emb_bank[t % 3][:, 0:E], patches[:, t, kc], proj_w[:, kc], start=kc == 0, stop=kc == KE - 1)
                last.then_inc(emb_ps, 1)

            def tokens_T(c):
                pe.wait_ge(xq_ok, c * CH // P + 3)
                if c >= 1:
                    pe.wait_ge(xqT_ok, c)
                for x in range(3):
                    t = c * CH // P + x
                    for h in range(2):
                        last = nc.tensor.transpose(xqT_bank[:, h, x * P:(x + 1) * P], xq[:, t, h * EC:(h + 1) * EC], identb[:])
                last.then_inc(xqT_ps, 1)

            def linear(x):
                kind, c, n = x
                j = lin_no[x]
                bank = lin_bank[j % 2]
                if j >= 2:
                    pe.wait_ge(lin_int, j - 1)
                if n == 0:
                    pe.wait_ge(xqT_ok, c + 1)
                    pe.wait_ge(w_quant, {"q": 2, "k": 4, "v": 6}[kind])
                for half in range(2):
                    for kc in range(2):
                        if kind == "v":
                            p, w0 = c * PPC + n, 2 * INNER + half * INNER // 2
                            last = mm(bank[:, half, 0:INNER // 2], xqT[:, kc, 2 * p:2 * p + 2, :].rearrange("p i n -> p (i n)"),
                                      ww1q[:, kc, w0:w0 + INNER // 2], start=kc == 0, stop=kc == 1)
                        else:
                            m = 2 * n + half + (HB if kind == "k" else 0)
                            last = mm(bank[:, half, 0:CH], ww1q[:, kc, m * P:(m + 1) * P],
                                      xqT[:, kc, c * CI:(c + 1) * CI, 0:NTOK], start=kc == 0, stop=kc == 1)
                last.then_inc(lin_ps, 1)

            def scores(p):
                c, r = divmod(p, PPC)
                if r == 0:
                    pe.wait_ge(q_ok, 4 * c + 4)
                    pe.wait_ge(k_ok, c + 1)
                for par in range(2):
                    i = 2 * r + par
                    cols = slice(i * NTOK, (i + 1) * NTOK)
                    for g in range(G3):
                        for tri in range(2):
                            s0 = ((par * G3 + g) * 2 + tri) * NTOK
                            for x in range(2):
                                part = 2 * tri + x
                                q0 = ((c % 2 * G3 + g) * CI + i) * 4 * TR + part * TR
                                last = mm(score_bank[:, s0:s0 + NTOK], q[:, q0:q0 + P],
                                          k[:, c % 2, TRI * g + tri + x, cols], start=x == 0, stop=x == 1)
                last.then_inc(s_ps, 1)

            def probs_T(p):
                pe.wait_ge(aq_ok, p + 1)
                if p >= 1:
                    pe.wait_ge(aT_ok, p)
                pe.wait_ge(xqT_ok, min(max(2, p + 2), CHUNKS))
                dst = probT_bank[:, 0:HT // 2].bitcast(BF16)
                for n in range(TRIS):
                    for par in range(2):
                        sg = par * TRIS + n
                        last = nc.tensor.transpose(dst[64 * par:64 * par + NTOK, n * TR:(n + 1) * TR],
                                                   aq[0:TR, p % 2, sg * NTOK:(sg + 1) * NTOK], identb[0:TR, 0:TR])
                last.then_inc(aT_ps, 1)

            def attend(p):
                pe.wait_ge(aT_ok, p + 1)
                pe.wait_ge(v_ok, p + 1)
                if p >= 1:
                    pe.wait_ge(o_int, p)
                for t in tiles_at(p + 1, 3):
                    pe.wait_ge(xnT_ok, t + 1)
                for m in range(HB):
                    for hp in range(2):
                        for par in range(2):
                            rows = slice(64 * par, 64 * par + NTOK)
                            h = 2 * m + hp
                            last = mm(head_bank[64 * hp:64 * hp + 64, par, m * NTOK:(m + 1) * NTOK],
                                      v[rows, p % VB, h * DH:(h + 1) * DH],
                                      aT[rows, p % 2, h * NTOK:(h + 1) * NTOK], start=True, stop=True)
                last.then_inc(o_ps, 1)

            def project(t):
                if t >= 1:
                    pe.wait_ge(h2_ok, t)
                pe.wait_ge(dif_ok, min(5 + 2 * t, PAIRS))
                pe.wait_ge(o_ok, -(-(t + 1) * P // (4 * NTOK)))
                pe.wait_ge(w_quant, len(WCH))
                for m in range(HB):
                    last = mm(proj_bank, oT[:, m, t * P:(t + 1) * P], ww2q[:, m], start=m == 0,
                              stop=m == HB - 1)
                last.then_inc(pr_ps, 1)

            def norm_T(t):
                if t >= 1:
                    pe.wait_ge(xnT_ok, t)
                pe.wait_ge(xn_ok, t + 1)
                for c in range(2):
                    last = nc.tensor.transpose(xnT_bank[0:EC, c * P:(c + 1) * P],
                                               xn[:, t % 2, c * EC:(c + 1) * EC], ident[:])
                last.then_inc(xnT_ps, 1)

            def gate(t):
                pe.wait_ge(xnT_ok, t + 1)
                pe.wait_ge(gate_in, 32)
                for c in range(2):
                    last = mm(gate_bank[:, t * NEXP:(t + 1) * NEXP], xnT[:, t % 2, c], gate_w[:, c],
                              start=c == 0, stop=c == 1)
                last.then_inc(gate_ps, 1)

            pe.wait_ge(proj_in, 16)
            pe.wait_ge(psum_clear, 1)
            for t in range(TT):
                embed(t)
                if t == 4:
                    pe.wait_ge(ident_ok, 3)
                    tokens_T(0)
                if t == 5:
                    for x in lin_groups(-1)[:QG]:
                        linear(x)
                if t == 6:
                    for x in lin_groups(-1)[QG:]:
                        linear(x)
                    tokens_T(1)
            pe.wait_ge(h_ok, TT)
            scores(0)
            for i in range(STEPS):
                if i + 1 < PAIRS:
                    pe.wait_ge(dif_ok, i + 1)
                    for t in tiles_at(i, 1):
                        pe.wait_ge(h2_ok, t + 1)
                    scores(i + 1)
                for x in lin_groups(i)[:1]:
                    linear(x)
                if 2 <= i < CHUNKS:
                    pe.wait_ge(aT_ok, i - 1)
                    tokens_T(i)
                for t in tiles_at(i, 0):
                    project(t)
                if 0 <= i - 2 < PAIRS:
                    attend(i - 2)
                for x in lin_groups(i)[1:]:
                    linear(x)
                if 0 <= i - 1 < PAIRS:
                    probs_T(i - 1)
                if tiles_at(i, 4) + tiles_at(i, 3):
                    pe.wait_ge(o_int, min(i - 1, PAIRS))
                for t in tiles_at(i, 4):
                    gate(t)
                for t in tiles_at(i, 3):
                    norm_T(t)

            pe.wait_ge(onehot_ok, 1)
            pe.wait_ge(const_ok, NCONST)
            pe.wait_ge(xnT_ok, TT)
            count = lin_bank[0][:, 0, 0:(TT + 1) * NEXP]
            mm(count, before[:], onehot[:].rearrange("p t e -> p (t e)"), start=True, stop=False)
            for t in range(TT):
                last = mm(count[:, (t + 1) * NEXP:].rearrange("p (t e) -> p t e", e=NEXP), ones[:],
                          onehot[:, t:t + 1].to_broadcast([P, TT - t, NEXP]), start=False, stop=t == TT - 1)
            last.then_inc(count_ps, 1)

            def slots_T(j):
                pe.wait_ge(xs_in[j], 16)
                if j >= 2:
                    pe.wait_ge(slotT_ok, j - 1)
                out = slotT_bank[j % 2][0:EC, 0:2 * P].bitcast(F16).rearrange("p (s n) -> p s n", s=4)
                for s in range(4):
                    last = nc.tensor.transpose(out[:, s], xs16[:, j, 2 * E + s * EC:2 * E + (s + 1) * EC], identh[:])
                last.then_inc(slotT_ps, 1)

            PARTS = [(0, 0), (0, 1), (1, 0)]

            def up(j, e):
                pe.wait_ge(slotT_ok, j + 1)
                for m in range(HM):
                    n = j * HM + m
                    if n >= 4:
                        pe.wait_ge(g_ok, n - 3)
                    for x, (sw, sx) in enumerate(PARTS):
                        for c in range(2):
                            last = mm(up_bank[n % 4][:, 0:P], w1[:, bass.ds(e, 1), sw, c, m * P:(m + 1) * P].rearrange(
                                          "p e n -> p (e n)"), xT[:, j % 3, 2 * sx + c],
                                      start=x == 0 and c == 0, stop=x == 2 and c == 1)
                    last.then_inc(up_ps, 1)

            def down(j, e):
                pe.wait_ge(glo_ok, j + 1)
                if j >= 2:
                    pe.wait_ge(y_ok, j - 1)
                for m in range(HM):
                    we = w2[:, bass.ds(e, 1), m].rearrange("p e s n -> p (e s n)")
                    mm(down_bank[j % 2][:, 0:2 * E], gs[:, j % 2, 0, m], we, start=m == 0, stop=False)
                    last = mm(down_bank[j % 2][:, 0:E], gs[:, j % 2, 1, m], we[:, 0:E], start=False, stop=m == HM - 1)
                last.then_inc(down_ps, 1)

            pe.wait_ge(wlo_ok, len(SPLITS))
            pe.wait_ge(expert_ok, 1)
            experts = [pe.value_load(expert[0:1, j:j + 1], min_val=0, max_val=NEXP - 1) for j in range(SLOT_TILES)]
            slots_T(0)
            slots_T(1)
            for j, e in enumerate(experts):
                up(j, e)
                if j + 2 < SLOT_TILES:
                    slots_T(j + 2)
                if j >= 1:
                    down(j - 1, experts[j - 1])
            down(SLOT_TILES - 1, experts[-1])


_OUT = ((32, 36, 192), "float32")


def kernel(**inputs):
    import numpy as np
    import concourse.bacc as bacc
    from concourse.bass_utils import run_bass_kernel_spmd

    a = {k: np.asarray(x) for k, x in inputs.items()}
    imgs, cin, hh, ww = a["x"].shape
    ps = 16
    kdim = cin * ps * ps
    tok = imgs * (hh // ps) * (ww // ps)
    emb = a["L0_tok_proj_w"].shape[0]
    inner = a["L0_attn_ww2"].shape[1]
    nexp, _, hid = a["L0_ffn_W1"].shape
    x = a["x"].reshape(imgs, cin, hh // ps, ps, ww // ps, ps).transpose(1, 3, 5, 0, 2, 4)
    x = x.reshape(kdim // 128, 128, tok // 128, 128).transpose(1, 2, 0, 3)
    names = ("x1", "w1", "q", "k", "a", "v", "x2", "w2")
    quant = np.concatenate([a[f"L0_attn_s{n}"].reshape(1) for n in names] +
                           [a[f"L0_attn_z{n}"].reshape(1) for n in names])

    def rows(w, r):
        return w.reshape(w.shape[0] // r, r, w.shape[1]).transpose(1, 0, 2)

    arrays = {
        "patches": x,
        "proj_w": rows(a["L0_tok_proj_w"].T, 128),
        "proj_b": a["L0_tok_proj_b"],
        "quant": quant,
        "ww1": rows(a["L0_attn_ww1"].T, emb // 2),
        "ww2": rows(a["L0_attn_ww2"].T, 128),
        "bb2": a["L0_attn_bb2"],
        "gate_w": rows(a["L0_ffn_Wg"], emb // 2),
        "gate_b": a["L0_ffn_bg"],
        "w1": a["L0_ffn_W1"].reshape(nexp, 2, emb // 2, hid).transpose(2, 0, 1, 3),
        "b1": a["L0_ffn_b1"].reshape(nexp, hid // 128, 128).transpose(2, 0, 1),
        "w2": a["L0_ffn_W2"].reshape(nexp, hid // 128, 128, emb).transpose(2, 0, 1, 3),
        "b2": a["L0_ffn_b2"],
    }
    nc = bacc.Bacc("TRN2", target_bir_lowering=False, num_devices=1)
    args, sent = [], {}
    for name, arr in arrays.items():
        sent[f"in_{name}"] = np.ascontiguousarray(arr)
        args.append(nc.dram_tensor(f"in_{name}", arr.shape, mybir.dt.from_np(arr.dtype), kind="ExternalInput").ap())
    args.append(nc.dram_tensor("out_0", (tok, emb), F32, kind="ExternalOutput").ap())
    vit_kernel(nc, *args)
    r = run_bass_kernel_spmd(nc, [sent], core_ids=[0])
    return r.results[0]["out_0"].reshape(_OUT[0])
```

```python
from contextlib import ExitStack

import concourse.bass as bass
from concourse import mybir

F32 = mybir.dt.float32
BF16 = mybir.dt.bfloat16
F16 = mybir.dt.float16
I16 = mybir.dt.int16
I32 = mybir.dt.int32
U32 = mybir.dt.uint32
ALU = mybir.AluOpType
ACT = mybir.ActivationFunctionType
AX = mybir.AxisListType

P = 128
ROUND = 1.5 * 2.0 ** 23
QMAX = 15.0
EPS = 1e-5
WSCALE = 64.0
YB = 4
NCONST = 3 + 4 + 3 + 4 + 12
X1, W1Q, QQ, KQ, AQ, VQ, X2, W2Q = range(8)


def vit_kernel(nc, patches_d, proj_w_d, proj_b_d, quant_d, ww1_d, ww2_d, bb2_d,
               gate_w_d, gate_b_d, w1_d, b1_d, w2_d, b2_d, out_d):
    _, TT, KE, _ = patches_d.shape
    T = TT * P
    E = proj_w_d.shape[2]
    EC = E // 2
    TAIL = E - P
    NTOK = 36
    IMGS = T // NTOK
    PAIRS = IMGS // 2
    HEADS, DH = 12, 64
    INNER = HEADS * DH
    HB = INNER // P
    _, NEXP, HM = b1_d.shape
    HID = HM * P
    CH = 288
    CI = CH // NTOK
    CHUNKS = T // CH
    PPC = PAIRS // CHUNKS
    HT = HEADS * NTOK
    TRI = 3
    TR = TRI * NTOK
    TRIS = HEADS // TRI
    G3 = HEADS // (2 * TRI)
    SG = 2 * TRIS
    SLOT_TILES = (T + NEXP * (P - 1)) // P
    SLOTS = SLOT_TILES * P
    PICKED = 2
    ROW = 2 * E + 4
    QG, VG = HB // 2, PPC

    with ExitStack() as ctx:
        def sb(name, shape, dt=F32):
            return ctx.enter_context(nc.sbuf_tensor(name, shape, dt))

        def sem(name):
            return ctx.enter_context(nc.semaphore(name))

        def psum(name, shape):
            return ctx.enter_context(nc.psum_tensor(name, shape, F32))

        lin_bank = [psum(f"lin_bank{i}", [P, 2, 512]) for i in range(2)]
        score_bank = psum("score_bank", [P, 512])
        probT_bank = psum("probT_bank", [P, 512])
        head_bank = psum("head_bank", [P, 2, 512])
        proj_bank = [score_bank[:, SG * NTOK:SG * NTOK + E]] * (TT - 1) + [lin_bank[0][:, 0, 0:E]]
        xnT_bank = [probT_bank[:, 256:512]] * (TT - 1) + [lin_bank[1][:, 0, 0:256]]
        gate_bank = head_bank[:, 1, HT:HT + TT * 4]
        emb_bank = [head_bank[:, 0], head_bank[:, 1], score_bank[:]]
        xqT_bank = probT_bank[0:EC].bitcast(BF16)[:, 0:2 * 3 * P].rearrange("p (c n) -> p c n", c=2)
        up_bank = [lin_bank[i // 2][:, i % 2] for i in range(4)]
        slotT_bank = [score_bank[:], probT_bank[:]]
        down_bank = [head_bank[:, 0], head_bank[:, 1]]

        patches = sb("patches", [P, TT, KE, P])
        proj_w = sb("proj_w", [P, KE, E])
        proj_b = sb("proj_b", [P, E])
        bb2 = sb("bb2", [P, E])
        quant = sb("quant", [P, 16])
        early = sb("early", [P, 6 * INNER])
        ww1 = early[0:EC].rearrange("p (c n) -> p c n", c=2)
        ww1q = sb("ww1q", [EC, 2, 3 * INNER], BF16)
        ww2 = sb("ww2", [P, HB, E])
        ww2q = sb("ww2q", [P, HB, E], BF16)
        inv = sb("inv", [P, 8])
        zr = sb("zr", [P, 8])
        lo = sb("lo", [P, 8])
        hi = sb("hi", [P, 8])
        fac = sb("fac", [P, 8])
        sxw, rq, rk, rv, cexp, ro, so, tmp = (fac[:, i:i + 1] for i in range(8))
        ident = sb("ident", [P, P])
        identb = sb("identb", [P, P], BF16)
        identh = sb("identh", [P, P], F16)
        before = sb("before", [P, P], BF16)
        ones = sb("ones", [P, P], BF16)
        row = sb("row", [P, TT, ROW])
        row16 = row[:].rearrange("p t n -> p (t n)").bitcast(F16).rearrange("p (t n) -> p t n", t=TT)
        blank = sb("blank", [P, ROW])
        stats = sb("stats", [P, 2, 6])
        mv = sb("mv", [P, TT, 2])
        veps = sb("veps", [P, TT])
        rstd = sb("rstd", [P, TT])
        rscale = sb("rscale", [P, TT])
        nhalf = sb("nhalf", [P, 1])
        xint = sb("xint", [P, 2, E], I16)
        xq = sb("xq", [P, TT, E], BF16)
        xqT = sb("xqT", [EC, 2, IMGS, DH], BF16)
        qkint = sb("qkint", [P, 2 * HB, CH], I16)
        QROW = G3 * CI * 4 * TR
        q = sb("q", [P, 2, QROW + P - TR], BF16)
        q_slots = q[:, :, 0:QROW].rearrange("p b (g i s n) -> p b g i s n", g=G3, i=CI, n=NTOK)
        k = sb("k", [P, 2, HB, CH], BF16)
        vint = sb("vint", [P, 2, INNER], I16)
        wint = vint
        VB = 2 * PPC - 1
        v = sb("v", [P, VB, INNER], BF16)
        mx = sb("mx", [P, 2, SG])
        den = sb("den", [P, 2, SG])
        dens = sb("dens", [P, 2, SG])
        rden = sb("rden", [P, 2, SG])
        dif = sb("dif", [P, 2, SG * NTOK])
        ex = sb("ex", [P, 2, SG * NTOK])
        aint = sb("aint", [P, 2, SG * NTOK], I16)
        aq = sb("aq", [P, 2, SG * NTOK], BF16)
        aT = sb("aT", [P, 2, HT], BF16)
        oint = sb("oint", [P, 2, HB, 4 * NTOK], I16)
        oT = sb("oT", [P, HB, T], BF16)
        xn = sb("xn", [P, 2, E])
        xnT = sb("xnT", [EC, 2, 2, P])
        gate_w = sb("gate_w", [EC, 2, NEXP])
        gate_b = sb("gate_b", [P, NEXP])
        prio = sb("prio", [P, NEXP])
        earlier = sb("earlier", [P, NEXP, NEXP])
        tile_no = sb("tile_no", [P, SLOT_TILES])
        logit = sb("logit", [P, TT, NEXP])
        isbest = sb("isbest", [P, TT, NEXP])
        best = sb("best", [P, TT])
        onehot = sb("onehot", [P, TT + 1, NEXP], BF16)
        ntile = sb("ntile", [P, NEXP])
        first = sb("first", [P, NEXP])
        prod = sb("prod", [P, NEXP, NEXP])
        place = sb("place", [P, TT, NEXP])
        slot = sb("slot", [P, TT], I32)
        started = sb("started", [P, SLOT_TILES, NEXP])
        expert = sb("expert", [P, SLOT_TILES], I32)
        expert_f = sb("expert_f", [P, SLOT_TILES])
        slot_f = sb("slot_f", [P, TT])
        b1 = sb("b1", [P, NEXP, HM])
        b2 = sb("b2", [P, NEXP, E])
        w1 = sb("w1", [P, NEXP, 3, HID], F16)
        w2 = early[:].bitcast(F16).rearrange("p (e m s n) -> p e m s n", e=NEXP, s=2, m=HM)
        warm = sb("warm", [1, 1])
        flat = patches[:].rearrange("p t k n -> p (t k n)")
        w1f = flat[:, 0:NEXP * 2 * HID].rearrange("p (e c n) -> p e c n", e=NEXP, c=2)
        w2f = flat[:, 0:NEXP * 2 * HID].rearrange("p (e n) -> p e n", e=NEXP)[:, :, 0:HM * E].rearrange(
            "p e (m n) -> p e m n", m=HM)
        nx = SLOT_TILES * ROW
        xs = flat[:, 0:nx].rearrange("p (j n) -> p j n", n=ROW)
        xs16 = flat[:, 0:nx].bitcast(F16).rearrange("p (j n) -> p j n", n=2 * ROW)
        late = q[:].rearrange("p b n -> p (b n)").bitcast(F32)
        gs = late[:, 0:2 * HID].bitcast(F16).rearrange("p (b s m n) -> p b s m n", b=2, s=2, m=HM)
        x0 = 2 * HID
        xT = late[:, x0:x0 + 3 * 2 * P].bitcast(F16).rearrange("p (b s n) -> p b s n", b=3, s=4)
        y0 = x0 + 3 * 2 * P
        yo = late[:, y0:y0 + YB * E].rearrange("p (b n) -> p b n", b=YB)
        hres = late[:, y0 + YB * E:y0 + (YB + 2) * E].rearrange("p (b n) -> p b n", b=2)
        g0 = y0 + (YB + 2) * E
        g = late[:, g0:g0 + 2 * HID].rearrange("p (b m n) -> p b m n", b=2, m=HM)
        p0 = g0 + 2 * HID
        picked = late[:, p0:p0 + PICKED * TT * P // 2].bitcast(F16).rearrange("p (j t n) -> p j t n", j=PICKED, t=TT)
        slot_int, slot_no = dif[:, 0, 0:PICKED * P].bitcast(I32), dif[:, 1, 0:PICKED * P]
        slots_d = nc.dram_tensor("slots", (SLOTS, ROW), F32).ap()

        (quant_in, proj_in, bias_in, bb2_in, ww1_in, ww2_in, gate_in, w1_in, b12_in, blank_out,
         scattered) = map(sem, (
             "quant_in", "proj_in", "bias_in", "bb2_in", "ww1_in", "ww2_in", "gate_in", "w1_in", "b12_in",
             "blank_out", "scattered"))
        stored = [sem(f"stored{b}") for b in range(YB)]
        w2_in = [sem(f"w2_in{e}") for e in range(NEXP)]
        patch_in = [sem(f"patch_in{t}") for t in range(TT)]
        xs_in = [sem(f"xs_in{j}") for j in range(SLOT_TILES)]
        pool_step, ident_ok, pad_ok, qpad_ok, blank_ok, const_ok, setup, scales_ok, psum_clear = map(sem, (
            "pool_step", "ident_ok", "pad_ok", "qpad_ok", "blank_ok", "const_ok", "setup", "scales_ok", "psum_clear"))
        w_int, w_quant, emb_ps, h_ok, stat_ok, aggr_ok, var_ok, rstd_ok, rscale_ok, norm_ok, xq_ok = map(sem, (
            "w_int", "w_quant", "emb_ps", "h_ok", "stat_ok", "aggr_ok", "var_ok", "rstd_ok", "rscale_ok",
            "norm_ok", "xq_ok"))
        hb_ok, xqT_ps, xqT_ok = map(sem, ("hb_ok", "xqT_ps", "xqT_ok"))
        lin_ps, lin_int, q_ok, k_ok, v_ok = map(sem, ("lin_ps", "lin_int", "q_ok", "k_ok", "v_ok"))
        s_ps, mx_ok, dif_ok, ex_ok, den_ok, dens_ok, rden_ok, aint_ok, aq_ok = map(sem, (
            "s_ps", "mx_ok", "dif_ok", "ex_ok", "den_ok", "dens_ok", "rden_ok", "aint_ok", "aq_ok"))
        aT_ps, aT_ok, o_ps, o_int, o_ok = map(sem, ("aT_ps", "aT_ok", "o_ps", "o_int", "o_ok"))
        pr_ps, h2_ok, xn_ok, xhi_ok, xlo_ok, xnT_ps, xnT_ok, gate_ps = map(sem, (
            "pr_ps", "h2_ok", "xn_ok", "xhi_ok", "xlo_ok", "xnT_ps", "xnT_ok", "gate_ps"))
        wscaled, whi_ok, wlo_ok, route, onehot_ok, count_ps, slot_ok, expert_ok, picked_ok, slot_no_ok = map(sem, (
            "wscaled", "whi_ok", "wlo_ok", "route", "onehot_ok", "count_ps", "slot_ok", "expert_ok", "picked_ok", "slot_no_ok"))
        slotT_ps, slotT_ok, up_ps, g_ok, ghi_ok, glo_ok, down_ps, res_ok, y_ok = map(sem, (
            "slotT_ps", "slotT_ok", "up_ps", "g_ok", "ghi_ok", "glo_ok", "down_ps", "res_ok", "y_ok"))

        STEPS = PAIRS + 7

        def lin_groups(i):
            if i == -1:
                return [("q", 0, n) for n in range(QG)] + [("k", 0, n) for n in range(QG)]
            out = []
            c, r = divmod(i, PPC)
            if i < 2:
                out += [("v", 0, n) for n in range(i * VG // 2, (i + 1) * VG // 2)]
            if c + 1 < CHUNKS:
                if r == 0:
                    out += [("q", c + 1, n) for n in range(QG)]
                if r == 1:
                    out += [("k", c + 1, n) for n in range(QG)]
                if r >= 2:
                    out += [("v", c + 1, n) for n in range((r - 2) * VG // 2, (r - 1) * VG // 2)]
            return out

        def tiles_at(i, delay):
            return [t for t in range(TT) if i - delay == 4 + min(2 * t, PAIRS - 2)]

        lin_no, lin_order = {}, []
        for i in range(-1, STEPS):
            for x in lin_groups(i):
                lin_no[x] = len(lin_order)
                lin_order.append(x)

        SPLITS = [(1, e, c) for e in range(NEXP) for c in range(2)] + [(2, e, c) for e in range(NEXP) for c in range(2)]
        EARLY = 2 * NEXP

        def split_views(n):
            which, e, c = SPLITS[n]
            if which == 1:
                return w1f[:, e, c], w1[:, e, 2 * c], w1[:, e, 1 + c]
            ms = slice(c * HM // 2, (c + 1) * HM // 2)
            return w2f[:, e, ms], w2[:, e, ms, 0], w2[:, e, ms, 1]

        def lists_after(j):
            if j < PICKED - 1:
                return []
            return range(PICKED if j == PICKED - 1 else j + 2, min(j + 3, SLOT_TILES))

        WCH = [(s, c) for s in range(3) for c in range(2)] + [(3, c) for c in range(2)]

        def weight_views(n):
            s, c = WCH[n]
            if s < 3:
                cols = slice(s * INNER, (s + 1) * INNER)
                return W1Q, ww1[:, c, cols], wint[0:EC, n % 2], ww1q[:, c, cols]
            ms = slice(c * HB // 2, (c + 1) * HB // 2)
            return W2Q, ww2[:, ms], wint[:, n % 2, 0:HB // 2 * E].rearrange("p (m n) -> p m n", n=E), ww2q[:, ms]

        def load_experts(engine):
            return nc.values_load_multi_w_load_instructions(expert[0:1, :], engines=[engine], min_val=0, max_val=NEXP - 1,
                                                            skip_runtime_bounds_check_because=(
                                                                "between one and all experts have started at a tile"))[1]

        def groups(x):
            return x.rearrange("p (h n) -> p h n", n=NTOK)

        block = ctx.enter_context(nc.Block())

        @block.sync
        def _(sp):
            sp.dma_start(quant[:], quant_d.partition_broadcast(P)).then_inc(quant_in, 16)
            sp.dma_start(proj_w[:], proj_w_d).then_inc(proj_in, 16)
            for t in range(TT):
                sp.dma_start(patches[:, t], patches_d[:, t]).then_inc(patch_in[t], 16)
                if t == 0:
                    sp.dma_start(proj_b[:], proj_b_d.partition_broadcast(P)).then_inc(bias_in, 16)
                    sp.dma_start(bb2[:], bb2_d.partition_broadcast(P)).then_inc(bb2_in, 16)
                if t == 2:
                    sp.dma_start(ww1, ww1_d).then_inc(ww1_in, 16)
            sp.dma_start(ww2[:], ww2_d).then_inc(ww2_in, 16)
            sp.dma_start(gate_w[:], gate_w_d).then_inc(gate_in, 16)
            sp.dma_start(gate_b[:], gate_b_d.partition_broadcast(P)).then_inc(gate_in, 16)
            sp.wait_ge(emb_ps, TT)
            sp.dma_start(w1f[:, :, 0], w1_d[0:P]).then_inc(w1_in, 16)
            for half in range(2):
                sp.dma_start(w1f[half * TAIL:(half + 1) * TAIL, :, 1], w1_d[P:E]).then_inc(w1_in, 16)
            sp.dma_start(b1[:], b1_d).then_inc(b12_in, 16)
            sp.dma_start(b2[:], b2_d.rearrange("e n -> (e n)").partition_broadcast(P)).then_inc(b12_in, 16)
            sp.wait_ge(blank_ok, 2)
            for j in range(SLOT_TILES):
                sp.dma_start(slots_d[j * P:(j + 1) * P, :], blank[:]).then_inc(blank_out, 16)
            for e in range(NEXP):
                sp.wait_ge(wlo_ok, 2 * e + 2)
                sp.dma_start(w2f[:, e], w2_d[:, e]).then_inc(w2_in[e], 16)
            sp.wait_ge(wlo_ok, len(SPLITS))
            sp.wait_ge(scattered, 16 * TT)
            for j in [PICKED] + [j for j in range(SLOT_TILES) if j != PICKED]:
                sp.dma_start(xs[:, j], slots_d[j * P:(j + 1) * P, :]).then_inc(xs_in[j], 16)

        @block.gpsimd
        def _(pool):
            gp = nc.gpsimd
            steps = [0]

            def step(ins):
                steps[0] += 1
                ins.then_inc(pool_step, 1)
                pool.wait_ge(pool_step, steps[0])

            step(gp.memset(ident[:], 0.0))
            step(gp.affine_select(out=ident[:], in_=ident[:], compare_op=ALU.not_equal, fill=1.0, base=0,
                                  pattern=[[-1, P]], channel_multiplier=1))
            gp.tensor_copy(identb[:], ident[:]).then_inc(ident_ok, 1)
            gp.tensor_copy(identh[:], ident[:]).then_inc(ident_ok, 1)
            gp.memset(nhalf[:], -0.5).then_inc(ident_ok, 1)
            gp.memset(xqT[:], 0.0).then_inc(pad_ok, 1)
            gp.memset(q[:].rearrange("p b n -> p (b n)").bitcast(U32), 0).then_inc(qpad_ok, 1)
            pool.wait_ge(ident_ok, 3)
            for t in range(TT):
                pool.wait_ge(var_ok, t + 1)
                gp.tensor_tensor(rstd[:, t:t + 1], veps[:, t:t + 1], nhalf[:], ALU.pow).then_inc(rstd_ok, 1)
            pool.wait_ge(bb2_in, 16)
            for t in range(TT):
                pool.wait_ge(norm_ok, t + 1)
                gp.tensor_tensor(row[:, t, 0:E], row[:, t, 0:E], bb2[:], ALU.add).then_inc(hb_ok, 1)
            step(gp.memset(blank[:, 0:2 * E], 0.0))
            gp.iota(blank[:, 2 * E:ROW].bitcast(I32), pattern=[[0, 4]], base=T, channel_multiplier=1).then_inc(blank_ok, 1)
            gp.iota(row[:, :, 2 * E:ROW].bitcast(I32), pattern=[[P, TT], [0, 4]], base=0,
                    channel_multiplier=1).then_inc(blank_ok, 1)
            step(gp.memset(before[:], 1.0))
            gp.affine_select(out=before[:], in_=before[:], compare_op=ALU.is_gt, fill=0.0, base=0,
                             pattern=[[1, P]], channel_multiplier=-1).then_inc(const_ok, 1)
            gp.memset(ones[:], 1.0).then_inc(const_ok, 1)
            gp.memset(onehot[:, TT], 0.0).then_inc(const_ok, 1)
            for e in range(NEXP):
                gp.memset(prio[:, e:e + 1], float(NEXP - e)).then_inc(const_ok, 1)
                if e:
                    gp.memset(earlier[:, e, 0:e], 1.0).then_inc(const_ok, 1)
                gp.memset(earlier[:, e, e:], 0.0).then_inc(const_ok, 1)
            for j in range(SLOT_TILES):
                gp.memset(tile_no[:, j:j + 1], float(j)).then_inc(const_ok, 1)
            def split(n):
                w, whi, wlo = split_views(n)
                gp.tensor_scalar(w, w, WSCALE, None, ALU.mult).then_inc(wscaled, 1)
                pool.wait_ge(wscaled, n + 1)
                gp.tensor_copy(whi, w).then_inc(whi_ok, 1)
                pool.wait_ge(whi_ok, n + 1)
                rows = slice(TAIL if SPLITS[n][2] else 0, P)
                gp.tensor_tensor(wlo[rows], w[rows], whi[rows], ALU.subtract).then_inc(wlo_ok, 1)
                pool.wait_ge(wlo_ok, n + 1)

            pool.wait_ge(w1_in, 48)
            split(0)
            split(1)
            for t in range(TT):
                if t + 2 < EARLY:
                    split(t + 2)
                pool.wait_ge(var_ok, TT + t + 1)
                gp.tensor_tensor(rstd[:, t:t + 1], veps[:, t:t + 1], nhalf[:], ALU.pow).then_inc(rstd_ok, 1)
            pool.wait_ge(ex_ok, PAIRS)
            step(gp.iota(slot_int, pattern=[[1, PICKED * P]], base=0, channel_multiplier=0))
            gp.tensor_copy(slot_no, slot_int).then_inc(slot_no_ok, 1)
            pool.wait_ge(blank_out, 16 * SLOT_TILES)
            pool.wait_ge(xlo_ok, TT)
            pool.wait_ge(xhi_ok, TT)
            pool.wait_ge(slot_ok, 1)
            for t in range(TT):
                gp.indirect_dma_start(out=slots_d, out_offset=bass.IndirectOffsetOnAxis(ap=slot[:, t:t + 1], axis=0),
                                      in_=row[:, t, :], in_offset=None,
                                      bounds_check=SLOTS - 1, oob_is_err=False).then_inc(scattered, 16)
            for j in range(SLOT_TILES):
                pool.wait_ge(y_ok, j + 1)
                gp.indirect_dma_start(out=out_d, out_offset=bass.IndirectOffsetOnAxis(
                                          ap=xs[:, j, 2 * E:2 * E + 1].bitcast(I32), axis=0),
                                      in_=yo[:, j % YB, :], in_offset=None,
                                      bounds_check=T - 1, oob_is_err=False).then_inc(stored[j % YB], 16)
            for b in range(YB):
                pool.wait_ge(stored[b], 16 * (SLOT_TILES // YB))

        @block.scalar
        def _(act):
            a = nc.scalar

            def weights(n):
                s, w, wi, _ = weight_views(n)
                if n >= 2:
                    act.wait_ge(w_quant, n - 1)
                a.activation(wi, w, ACT.Copy, scale=inv[0:w.shape[0], s:s + 1]).then_inc(w_int, 1)

            def tokens_T(c):
                act.wait_ge(xqT_ps, c + 1)
                off = c * CH % P
                a.copy(xqT[:, :, c * CI:(c + 1) * CI, 0:NTOK],
                       xqT_bank[:, :, off:off + CH].rearrange("p c (i n) -> p c i n", n=NTOK)).then_inc(xqT_ok, 1)

            def linear(x):
                kind, c, n = x
                j = lin_no[x]
                bank = lin_bank[j % 2]
                act.wait_ge(lin_ps, j + 1)
                if kind == "v":
                    p = c * PPC + n
                    if p == 0:
                        act.wait_ge(w_quant, len(WCH))
                    if p >= 2:
                        act.wait_ge(v_ok, p - 1)
                    a.activation(vint[:, p % 2].rearrange("p (s n) -> p s n", s=2), bank[:, :, 0:INNER // 2],
                                 ACT.Copy, scale=rv).then_inc(lin_int, 1)
                    return
                m = 2 * n
                if kind == "k":
                    m += HB
                if c >= 1 and n == 0:
                    act.wait_ge(q_ok if kind == "q" else k_ok, 4 * c if kind == "q" else c)
                a.activation(qkint[:, m:m + 2], bank[:, :, 0:CH], ACT.Copy,
                             scale=rq if kind == "q" else rk).then_inc(lin_int, 1)

            def split_high(n):
                act.wait_ge(w2_in[SPLITS[n][1]], 16)
                w, whi, _ = split_views(n)
                a.activation(whi, w, ACT.Copy, scale=WSCALE).then_inc(whi_ok, 1)

            act.wait_ge(scales_ok, 1)
            act.wait_ge(ww1_in, 16)
            act.wait_ge(pad_ok, 1)
            for n in range(4):
                weights(n)
            tokens_T(0)
            weights(4)
            for x in lin_groups(-1)[:QG]:
                linear(x)
            weights(5)
            for x in lin_groups(-1)[QG:]:
                linear(x)
            tokens_T(1)
            act.wait_ge(ww2_in, 16)
            weights(6)
            weights(7)
            for i in range(STEPS):
                if i < PAIRS:
                    b = i % 2
                    act.wait_ge(dif_ok, i + 1)
                    if i >= 2:
                        act.wait_ge(aint_ok, i - 1)
                    a.activation(ex[0:TR, b], dif[0:TR, b], ACT.Exp, scale=cexp[0:TR]).then_inc(ex_ok, 1)
                for x in lin_groups(i)[:1]:
                    linear(x)
                if 2 <= i < CHUNKS:
                    tokens_T(i)
                p = i - 2
                if 0 <= p < PAIRS:
                    act.wait_ge(o_ps, p + 1)
                    if p >= 4 and p % 2 == 0:
                        act.wait_ge(o_ok, p // 2 - 1)
                    dst = oint[:, p // 2 % 2, :, (p % 2) * 2 * NTOK:(p % 2 + 1) * 2 * NTOK]
                    for hp in range(2):
                        rows = slice(DH * hp, DH * hp + DH)
                        a.activation(dst[rows].rearrange("p m (r n) -> p r m n", r=2),
                                     head_bank[rows, :, 0:HT].rearrange("p r (m h n) -> p r m h n", m=HB, h=2)[:, :, :, hp],
                                     ACT.Copy, scale=ro[rows]).then_inc(o_int, 1)
                for x in lin_groups(i)[1:]:
                    linear(x)
                for t in tiles_at(i, 2):
                    act.wait_ge(xn_ok, t + 1)
                    a.copy(row16[:, t, 2 * E:3 * E], xn[:, t % 2]).then_inc(xhi_ok, 1)
                p = i - 1
                if 0 <= p < PAIRS:
                    act.wait_ge(aT_ps, p + 1)
                    if p >= 2:
                        act.wait_ge(o_ps, p - 1)
                    a.copy(aT[:, p % 2], probT_bank[:, 0:HT // 2].bitcast(BF16)).then_inc(aT_ok, 1)
                for t in tiles_at(i, 3):
                    act.wait_ge(xnT_ps, t + 1)
                    if t >= 2:
                        act.wait_ge(gate_ps, t - 1)
                    a.copy(xnT[:, t % 2], xnT_bank[t][0:EC].rearrange(
                        "p (c n) -> p c n", c=2)).then_inc(xnT_ok, 1)
            act.wait_ge(const_ok, 1)
            a.activation(warm[:], nhalf[0:1], ACT.Gelu)
            for n in range(EARLY, len(SPLITS)):
                split_high(n)
            act.wait_ge(b12_in, 32)
            act.wait_ge(expert_ok, 1)
            experts = load_experts(mybir.EngineType.Activation)
            for j, e in enumerate(experts):
                for m in range(HM):
                    n = j * HM + m
                    act.wait_ge(up_ps, n + 1)
                    if j >= 2 and m == 0:
                        act.wait_ge(glo_ok, 2 * (j - 1))
                    a.activation(g[:, j % 2, m], up_bank[n % 4][:, 0:P], ACT.Gelu, scale=1.0 / WSCALE,
                                 bias=b1[:, bass.ds(e, 1), m]).then_inc(g_ok, 1)

        @block.vector
        def _(dve):
            d = nc.vector
            steps = [0]

            def step(ins):
                steps[0] += 1
                ins.then_inc(setup, 1)
                dve.wait_ge(setup, steps[0])

            def mul(out, x, y):
                step(d.tensor_tensor(out, x, y, ALU.mult))

            d.memset(probT_bank[:], 0.0).then_inc(psum_clear, 1)
            dve.wait_ge(quant_in, 16)
            scl, zero = quant[:, 0:8], quant[:, 8:16]
            step(d.reciprocal(inv[:], scl))
            step(d.tensor_scalar(zr[:], zero, ROUND, ROUND, ALU.add, ALU.subtract))
            step(d.tensor_scalar(lo[:], zr[:], -1.0, None, ALU.mult))
            step(d.tensor_scalar(hi[:], zr[:], -1.0, QMAX, ALU.mult, ALU.add))
            mul(sxw, scl[:, X1:X1 + 1], scl[:, W1Q:W1Q + 1])
            mul(rq, sxw, inv[:, QQ:QQ + 1])
            mul(rk, sxw, inv[:, KQ:KQ + 1])
            mul(rv, sxw, inv[:, VQ:VQ + 1])
            mul(tmp, scl[:, QQ:QQ + 1], scl[:, KQ:KQ + 1])
            step(d.tensor_scalar(cexp, tmp, DH ** -0.5, None, ALU.mult))
            mul(tmp, scl[:, AQ:AQ + 1], scl[:, VQ:VQ + 1])
            mul(ro, tmp, inv[:, X2:X2 + 1])
            d.tensor_tensor(so, scl[:, X2:X2 + 1], scl[:, W2Q:W2Q + 1], ALU.mult).then_inc(scales_ok, 1)
            dve.wait_ge(scales_ok, 1)

            def clip(out, x, s, n=P, base=0):
                return d.tensor_scalar(out, x, lo[base:base + n, s:s + 1], hi[base:base + n, s:s + 1],
                                       ALU.max, ALU.min)

            def weights(n):
                s, w, wi, wq = weight_views(n)
                dve.wait_ge(w_int, n + 1)
                clip(wq, wi, s, w.shape[0]).then_inc(w_quant, 1)

            def moments(t, n):
                d.bn_stats(stats[:, n % 2], row[:, t, 0:E]).then_inc(stat_ok, 1)

            def variance(t, n):
                dve.wait_ge(stat_ok, n + 1)
                d.bn_aggr(mv[:, t], stats[:, n % 2]).then_inc(aggr_ok, 1)

            def guard(t, n):
                dve.wait_ge(aggr_ok, n + 1)
                d.tensor_scalar(veps[:, t:t + 1], mv[:, t, 1:2], EPS, None, ALU.add).then_inc(var_ok, 1)

            def token_scale(t):
                dve.wait_ge(rstd_ok, t + 1)
                d.tensor_tensor(rscale[:, t:t + 1], rstd[:, t:t + 1], inv[:, X1:X1 + 1], ALU.mult).then_inc(rscale_ok, 1)

            def round_tokens(t):
                dve.wait_ge(rscale_ok, t + 1)
                d.tensor_scalar(xint[:, t % 2], row[:, t, 0:E], mv[:, t, 0:1], rscale[:, t:t + 1],
                                ALU.subtract, ALU.mult).then_inc(norm_ok, 1)

            def clip_tokens(t):
                dve.wait_ge(norm_ok, t + 1)
                clip(xq[:, t], xint[:, t % 2], X1).then_inc(xq_ok, 1)

            def linear(x):
                kind, c, n = x
                dve.wait_ge(lin_int, lin_no[x] + 1)
                if kind == "q":
                    if c >= 2:
                        dve.wait_ge(s_ps, (c - 1) * PPC)
                    if c == 0:
                        dve.wait_ge(qpad_ok, 1)
                    for g in range(G3):
                        for upper in range(2):
                            rows = slice(DH * upper, DH * upper + DH)
                            clip(q_slots[rows, c % 2, g, :, upper:upper + 11:5], qkint[rows, TRI * g:TRI * (g + 1)].rearrange(
                                     "p t (i n) -> p i t n", n=NTOK), QQ, DH, DH * upper).then_inc(q_ok, 1)
                elif kind == "k":
                    if c >= 2:
                        dve.wait_ge(s_ps, (c - 1) * PPC)
                    clip(k[:, c % 2], qkint[:, HB:2 * HB], KQ).then_inc(k_ok, 1)
                else:
                    p = c * PPC + n
                    if p >= VB:
                        dve.wait_ge(o_ps, p - VB + 1)
                    clip(v[:, p % VB], vint[:, p % 2], VQ).then_inc(v_ok, 1)

            def clips_of(i):
                return [x for x in lin_groups(i) if x[0] == "v" or x[2] == QG - 1]

            def split_low(n):
                w, whi, wlo = split_views(n)
                dve.wait_ge(whi_ok, n + 1)
                d.scalar_tensor_tensor(wlo, w, WSCALE, whi, ALU.mult, ALU.subtract).then_inc(wlo_ok, 1)

            for t in range(TT):
                dve.wait_ge(emb_ps, t + 1)
                if t == 0:
                    dve.wait_ge(bias_in, 16)
                d.tensor_tensor(row[:, t, 0:E], emb_bank[t % 3][:, 0:E], proj_b[:], ALU.add).then_inc(h_ok, 1)
                if t >= 1:
                    token_scale(t - 1)
                dve.wait_ge(h_ok, t + 1)
                moments(t, t)
                if t >= 1:
                    round_tokens(t - 1)
                variance(t, t)
                if t >= 1:
                    clip_tokens(t - 1)
                guard(t, t)
                if t >= 2:
                    weights(t - 2)
                if t == 6:
                    linear(lin_groups(-1)[QG - 1])
                if t == 7:
                    linear(lin_groups(-1)[2 * QG - 1])
            token_scale(TT - 1)
            round_tokens(TT - 1)
            clip_tokens(TT - 1)
            for n in range(TT - 2, len(WCH)):
                weights(n)

            for i in range(STEPS):
                new, old = i < PAIRS, 0 <= i - 1 < PAIRS
                b, p = i % 2, i - 1
                ob = p % 2
                for t in tiles_at(i, 1):
                    dve.wait_ge(pr_ps, t + 1)
                if new:
                    dve.wait_ge(s_ps, i + 1)
                    d.tensor_reduce(mx[0:TR, b], groups(score_bank[0:TR, 0:SG * NTOK]), AX.X, ALU.max).then_inc(mx_ok, 1)
                if old:
                    dve.wait_ge(ex_ok, p + 1)
                    d.tensor_reduce(den[0:TR, ob], groups(ex[0:TR, ob]), AX.X, ALU.add).then_inc(den_ok, 1)
                if new:
                    dve.wait_ge(mx_ok, i + 1)
                    if i >= 2:
                        dve.wait_ge(ex_ok, i - 1)
                    d.tensor_tensor(groups(dif[0:TR, b]), groups(score_bank[0:TR, 0:SG * NTOK]),
                                    mx[0:TR, b].unsqueeze(2).to_broadcast([TR, SG, NTOK]),
                                    ALU.subtract).then_inc(dif_ok, 1)
                for t in tiles_at(i, 1):
                    dve.wait_ge(hb_ok, t + 1)
                    d.scalar_tensor_tensor(row[:, t, 0:E], proj_bank[t], so, row[:, t, 0:E],
                                           ALU.mult, ALU.add).then_inc(h2_ok, 1)
                n = i - 4
                if n >= 0 and n % 2 == 0 and n // 2 < PAIRS // 2:
                    n //= 2
                    dve.wait_ge(o_int, 4 * n + 4)
                    clip(oT[:, :, n * 4 * NTOK:(n + 1) * 4 * NTOK], oint[:, n % 2], X2).then_inc(o_ok, 1)
                if old:
                    dve.wait_ge(den_ok, p + 1)
                    d.tensor_scalar(dens[0:TR, ob], den[0:TR, ob], scl[0:TR, AQ:AQ + 1], None,
                                    ALU.mult).then_inc(dens_ok, 1)
                clipped = clips_of(i - 1) if i else []
                values = [x for x in clipped if x[0] == "v"]
                for x in values[:1]:
                    linear(x)
                if old:
                    dve.wait_ge(dens_ok, p + 1)
                    d.reciprocal(rden[0:TR, ob], dens[0:TR, ob]).then_inc(rden_ok, 1)
                if old:
                    dve.wait_ge(rden_ok, p + 1)
                    d.tensor_tensor(groups(aint[0:TR, ob]), groups(ex[0:TR, ob]),
                                    rden[0:TR, ob].unsqueeze(2).to_broadcast([TR, SG, NTOK]),
                                    ALU.mult).then_inc(aint_ok, 1)
                for x in values[1:]:
                    linear(x)
                if old:
                    dve.wait_ge(aint_ok, p + 1)
                    if p >= 2:
                        dve.wait_ge(aT_ps, p - 1)
                    clip(aq[0:TR, ob], aint[0:TR, ob], AQ, TR).then_inc(aq_ok, 1)
                for t in tiles_at(i, 1):
                    dve.wait_ge(h2_ok, t + 1)
                    moments(t, TT + t)
                for t in tiles_at(i, 3):
                    dve.wait_ge(xhi_ok, t + 1)
                    d.tensor_tensor(row16[:, t, 3 * E:4 * E], xn[:, t % 2], row16[:, t, 2 * E:3 * E],
                                    ALU.subtract).then_inc(xlo_ok, 1)
                for t in tiles_at(i, 1):
                    variance(t, TT + t)
                for x in clipped:
                    if x[0] != "v":
                        linear(x)
                for t in tiles_at(i, 1):
                    guard(t, TT + t)
                for t in tiles_at(i, 2):
                    dve.wait_ge(rstd_ok, TT + t + 1)
                    if t >= 2:
                        dve.wait_ge(xnT_ps, t - 1)
                        dve.wait_ge(xlo_ok, t - 1)
                    d.tensor_scalar(xn[:, t % 2], row[:, t, 0:E], mv[:, t, 0:1], rstd[:, t:t + 1],
                                    ALU.subtract, ALU.mult).then_inc(xn_ok, 1)

            routed = [0]

            def rstep(ins):
                routed[0] += 1
                ins.then_inc(route, 1)
                dve.wait_ge(route, routed[0])

            def each_expert(x, n=TT):
                return x.unsqueeze(2).to_broadcast([P, n, NEXP])

            def each_tile(x, n=TT):
                return x.unsqueeze(1).to_broadcast([P, n, NEXP])

            dve.wait_ge(gate_in, 32)
            dve.wait_ge(const_ok, NCONST)
            dve.wait_ge(gate_ps, TT)
            rstep(d.tensor_tensor(logit[:], gate_bank.rearrange("p (t e) -> p t e", e=NEXP),
                                  each_tile(gate_b[:]), ALU.add))
            rstep(d.tensor_reduce(best[:], logit[:], AX.X, ALU.max))
            rstep(d.tensor_tensor(isbest[:], logit[:], each_expert(best[:]), ALU.is_equal))
            rstep(d.tensor_tensor(logit[:], isbest[:], each_tile(prio[:]), ALU.mult))
            rstep(d.tensor_reduce(best[:], logit[:], AX.X, ALU.max))
            d.tensor_tensor(onehot[:, 0:TT], logit[:], each_expert(best[:]), ALU.is_equal).then_inc(onehot_ok, 1)
            dve.wait_ge(onehot_ok, 1)
            dve.wait_ge(count_ps, 1)
            counts = lin_bank[0][:, 0, 0:(TT + 1) * NEXP].rearrange("p (t e) -> p t e", e=NEXP)
            rstep(d.tensor_scalar(ntile[:], counts[:, TT], 1.0 / P, (P - 1) / 2 / P, ALU.mult, ALU.add))
            rstep(d.tensor_scalar(ntile[:], ntile[:], ROUND, ROUND, ALU.add, ALU.subtract))
            rstep(d.tensor_tensor(prod[:], earlier[:], each_tile(ntile[:], NEXP), ALU.mult))
            rstep(d.tensor_reduce(first[:], prod[:], AX.X, ALU.add))
            rstep(d.scalar_tensor_tensor(place[:], each_tile(first[:]), float(P), counts[:, 0:TT], ALU.mult, ALU.add))
            rstep(d.tensor_tensor(place[:], place[:], onehot[:, 0:TT], ALU.mult))
            rstep(d.tensor_reduce(slot_f[:], place[:], AX.X, ALU.add))
            d.tensor_copy(slot[:], slot_f[:]).then_inc(slot_ok, 1)
            rstep(d.tensor_tensor(started[:], each_expert(tile_no[:], SLOT_TILES), each_tile(first[:], SLOT_TILES),
                                  ALU.is_ge))
            rstep(d.tensor_reduce(expert_f[:], started[:], AX.X, ALU.add))
            d.tensor_scalar(expert[:], expert_f[:], -1.0, None, ALU.add).then_inc(expert_ok, 1)

            def pick(j):
                for t in range(TT):
                    d.tensor_scalar(picked[:, j, t], slot_no[:, j * P:(j + 1) * P], slot_f[:, t:t + 1], None,
                                    ALU.is_equal).then_inc(picked_ok, 1)

            dve.wait_ge(slot_no_ok, 1)
            for j in range(PICKED):
                pick(j)


            def slots_T(j):
                dve.wait_ge(slotT_ps, j + 1)
                if j >= 3:
                    dve.wait_ge(up_ps, (j - 2) * HM)
                bank = slotT_bank[j % 2]
                bank = bank if j < PICKED else bank[:, 0:2 * P].bitcast(F16)
                d.tensor_copy(xT[:, j % 3, 0:3], bank[:, 0:3 * P].rearrange("p (s n) -> p s n", s=3)).then_inc(slotT_ok, 1)
                d.tensor_copy(xT[0:TAIL, j % 3, 3], bank[0:TAIL, 3 * P:4 * P]).then_inc(slotT_ok, 1)

            rest = len(SPLITS) - EARLY
            for j in range(PICKED):
                for n in range(j * rest // PICKED, (j + 1) * rest // PICKED):
                    split_low(EARLY + n)
                slots_T(j)

            def finish(j):
                e = experts[j]
                if j < PICKED:
                    dve.wait_ge(xs_in[j], 16)
                d.tensor_tensor(hres[:, j % 2], xs[:, j, 0:E], b2[:, bass.ds(e, 1), :].rearrange("p e n -> p (e n)"),
                                ALU.add).then_inc(res_ok, 1)
                dve.wait_ge(res_ok, 2 * j + 1)
                dve.wait_ge(down_ps, j + 1)
                d.scalar_tensor_tensor(hres[:, j % 2], down_bank[j % 2][:, E:2 * E], 1.0 / WSCALE, hres[:, j % 2],
                                       ALU.mult, ALU.add).then_inc(res_ok, 1)
                dve.wait_ge(res_ok, 2 * j + 2)
                if j >= YB:
                    dve.wait_ge(stored[j % YB], 16 * (j // YB))
                d.scalar_tensor_tensor(yo[:, j % YB], down_bank[j % 2][:, 0:E], 1.0 / WSCALE, hres[:, j % 2],
                                       ALU.mult, ALU.add).then_inc(y_ok, 1)

            dve.wait_ge(expert_ok, 1)
            experts = load_experts(mybir.EngineType.DVE)
            dve.wait_ge(b12_in, 32)
            for j in range(SLOT_TILES):
                if j == PICKED - 1:
                    slots_T(PICKED)
                for half in range(2):
                    ms = slice(half * HM // 2, (half + 1) * HM // 2)
                    dve.wait_ge(g_ok, j * HM + ms.stop)
                    if j >= 2 and half == 0:
                        dve.wait_ge(down_ps, j - 1)
                    d.tensor_copy(gs[:, j % 2, 0, ms], g[:, j % 2, ms]).then_inc(ghi_ok, 1)
                    dve.wait_ge(ghi_ok, 2 * j + half + 1)
                    d.tensor_tensor(gs[:, j % 2, 1, ms], g[:, j % 2, ms], gs[:, j % 2, 0, ms],
                                    ALU.subtract).then_inc(glo_ok, 1)
                for n in lists_after(j):
                    if n > PICKED:
                        slots_T(n)
                if j >= 1:
                    finish(j - 1)
            finish(SLOT_TILES - 1)

        @block.tensor
        def _(pe):
            mm = nc.tensor.matmul

            def embed(t):
                pe.wait_ge(patch_in[t], 16)
                if t >= 3:
                    pe.wait_ge(h_ok, t - 2)
                for kc in range(KE):
                    last = mm(emb_bank[t % 3][:, 0:E], patches[:, t, kc], proj_w[:, kc], start=kc == 0, stop=kc == KE - 1)
                last.then_inc(emb_ps, 1)

            def tokens_T(c):
                pe.wait_ge(xq_ok, c * CH // P + 3)
                if c >= 1:
                    pe.wait_ge(xqT_ok, c)
                for x in range(3):
                    t = c * CH // P + x
                    for h in range(2):
                        last = nc.tensor.transpose(xqT_bank[:, h, x * P:(x + 1) * P], xq[:, t, h * EC:(h + 1) * EC], identb[:])
                last.then_inc(xqT_ps, 1)

            def linear(x):
                kind, c, n = x
                j = lin_no[x]
                bank = lin_bank[j % 2]
                if j >= 2:
                    pe.wait_ge(lin_int, j - 1)
                if n == 0:
                    pe.wait_ge(xqT_ok, c + 1)
                    pe.wait_ge(w_quant, {"q": 2, "k": 4, "v": 6}[kind])
                for half in range(2):
                    for kc in range(2):
                        if kind == "v":
                            p, w0 = c * PPC + n, 2 * INNER + half * INNER // 2
                            last = mm(bank[:, half, 0:INNER // 2], xqT[:, kc, 2 * p:2 * p + 2, :].rearrange("p i n -> p (i n)"),
                                      ww1q[:, kc, w0:w0 + INNER // 2], start=kc == 0, stop=kc == 1)
                        else:
                            m = 2 * n + half + (HB if kind == "k" else 0)
                            last = mm(bank[:, half, 0:CH], ww1q[:, kc, m * P:(m + 1) * P],
                                      xqT[:, kc, c * CI:(c + 1) * CI, 0:NTOK], start=kc == 0, stop=kc == 1)
                last.then_inc(lin_ps, 1)

            def scores(p):
                c, r = divmod(p, PPC)
                if r == 0:
                    pe.wait_ge(q_ok, 4 * c + 4)
                    pe.wait_ge(k_ok, c + 1)
                for par in range(2):
                    i = 2 * r + par
                    cols = slice(i * NTOK, (i + 1) * NTOK)
                    for g in range(G3):
                        for tri in range(2):
                            s0 = ((par * G3 + g) * 2 + tri) * NTOK
                            for x in range(2):
                                part = 2 * tri + x
                                q0 = (g * CI + i) * 4 * TR + part * TR
                                last = mm(score_bank[:, s0:s0 + NTOK], q[:, c % 2, q0:q0 + P],
                                          k[:, c % 2, TRI * g + tri + x, cols], start=x == 0, stop=x == 1)
                last.then_inc(s_ps, 1)

            def probs_T(p):
                pe.wait_ge(aq_ok, p + 1)
                if p >= 1:
                    pe.wait_ge(aT_ok, p)
                for t in tiles_at(p, 3):
                    pe.wait_ge(xnT_ok, t + 1)
                pe.wait_ge(xqT_ok, min(max(2, p + 2), CHUNKS))
                dst = probT_bank[:, 0:HT // 2].bitcast(BF16)
                for n in range(TRIS):
                    for par in range(2):
                        sg = par * TRIS + n
                        last = nc.tensor.transpose(dst[64 * par:64 * par + NTOK, n * TR:(n + 1) * TR],
                                                   aq[0:TR, p % 2, sg * NTOK:(sg + 1) * NTOK], identb[0:TR, 0:TR])
                last.then_inc(aT_ps, 1)

            def attend(p):
                pe.wait_ge(aT_ok, p + 1)
                pe.wait_ge(v_ok, p + 1)
                if p >= 1:
                    pe.wait_ge(o_int, 2 * p)
                for m in range(HB):
                    for hp in range(2):
                        for par in range(2):
                            rows = slice(64 * par, 64 * par + NTOK)
                            h = 2 * m + hp
                            last = mm(head_bank[:, par, h * NTOK:(h + 1) * NTOK],
                                      v[rows, p % VB, m * P:(m + 1) * P],
                                      aT[rows, p % 2, h * NTOK:(h + 1) * NTOK], start=True, stop=True)
                last.then_inc(o_ps, 1)

            def project(t):
                if 1 <= t < TT - 1:
                    pe.wait_ge(h2_ok, t)
                if t == TT - 1:
                    pe.wait_ge(lin_int, len(lin_order))
                pe.wait_ge(dif_ok, min(5 + 2 * t, PAIRS))
                pe.wait_ge(o_ok, -(-(t + 1) * P // (4 * NTOK)))
                pe.wait_ge(w_quant, len(WCH))
                for m in range(HB):
                    last = mm(proj_bank[t], oT[:, m, t * P:(t + 1) * P], ww2q[:, m], start=m == 0,
                              stop=m == HB - 1)
                last.then_inc(pr_ps, 1)

            def norm_T(t):
                if 1 <= t < TT - 1:
                    pe.wait_ge(xnT_ok, t)
                pe.wait_ge(xn_ok, t + 1)
                for c in range(2):
                    last = nc.tensor.transpose(xnT_bank[t][0:EC, c * P:(c + 1) * P],
                                               xn[:, t % 2, c * EC:(c + 1) * EC], ident[:])
                last.then_inc(xnT_ps, 1)

            def gate(t):
                pe.wait_ge(xnT_ok, t + 1)
                pe.wait_ge(gate_in, 32)
                for c in range(2):
                    last = mm(gate_bank[:, t * NEXP:(t + 1) * NEXP], xnT[:, t % 2, c], gate_w[:, c],
                              start=c == 0, stop=c == 1)
                last.then_inc(gate_ps, 1)

            pe.wait_ge(proj_in, 16)
            pe.wait_ge(psum_clear, 1)
            for t in range(TT):
                embed(t)
                if t == 4:
                    pe.wait_ge(ident_ok, 3)
                    tokens_T(0)
                if t == 5:
                    for x in lin_groups(-1)[:QG]:
                        linear(x)
                if t == 6:
                    for x in lin_groups(-1)[QG:]:
                        linear(x)
                    tokens_T(1)
            pe.wait_ge(h_ok, TT)
            scores(0)
            for i in range(STEPS):
                if i + 1 < PAIRS:
                    pe.wait_ge(dif_ok, i + 1)
                    for t in tiles_at(i, 1):
                        pe.wait_ge(h2_ok, t + 1)
                    scores(i + 1)
                for x in lin_groups(i)[:1]:
                    linear(x)
                if 2 <= i < CHUNKS:
                    pe.wait_ge(aT_ok, i - 1)
                    tokens_T(i)
                for t in tiles_at(i, 0):
                    project(t)
                if 0 <= i - 2 < PAIRS:
                    attend(i - 2)
                for x in lin_groups(i)[1:]:
                    linear(x)
                for t in tiles_at(i, 3):
                    pe.wait_ge(aT_ok, min(i - 1, PAIRS))
                    norm_T(t)
                if 0 <= i - 1 < PAIRS:
                    probs_T(i - 1)
                for t in tiles_at(i, 4):
                    pe.wait_ge(o_int, 2 * min(i - 1, PAIRS))
                    gate(t)

            pe.wait_ge(onehot_ok, 1)
            pe.wait_ge(const_ok, NCONST)
            pe.wait_ge(xnT_ok, TT)
            count = lin_bank[0][:, 0, 0:(TT + 1) * NEXP]
            mm(count, before[:], onehot[:].rearrange("p t e -> p (t e)"), start=True, stop=False)
            for t in range(TT):
                last = mm(count[:, (t + 1) * NEXP:].rearrange("p (t e) -> p t e", e=NEXP), ones[:],
                          onehot[:, t:t + 1].to_broadcast([P, TT - t, NEXP]), start=False, stop=t == TT - 1)
            last.then_inc(count_ps, 1)

            def pieces(x, j):
                hi, lo = x[:, j, 2 * E:3 * E], x[:, j, 3 * E:4 * E]
                return [(hi[:, 0:P], 0, P, 0), (lo[:, 0:P], 0, P, 1), (hi[:, P:E], 0, TAIL, 2), (hi[:, P:E], TAIL, P, 2),
                        (lo[:, P:E], 0, TAIL, 3)]

            def slots_T(j):
                pe.wait_ge(xs_in[j], 16)
                if j >= 2:
                    pe.wait_ge(slotT_ok, 2 * (j - 1))
                out = slotT_bank[j % 2][:, 0:2 * P].bitcast(F16).rearrange("p (s n) -> p s n", s=4)
                for x, r0, r1, s in pieces(xs16, j):
                    last = nc.tensor.transpose(out[r0:r1, s], x, identh[:])
                last.then_inc(slotT_ps, 1)

            def pick(j):
                pe.wait_ge(picked_ok, (j + 1) * TT)
                for n in range(5):
                    for t in range(TT):
                        x, r0, r1, s = pieces(row16, t)[n]
                        last = mm(slotT_bank[j % 2][r0:r1, s * P:(s + 1) * P], x,
                                  picked[:, j, t], start=t == 0, stop=t == TT - 1)
                last.then_inc(slotT_ps, 1)

            PASSES = [(0, 0, P), (0, 1, P), (1, 0, P), (2, 2, P), (2, 3, TAIL)]

            def up(j, m):
                n = j * HM + m
                if n >= 4:
                    pe.wait_ge(g_ok, n - 3)
                for x, (part, piece, rows) in enumerate(PASSES):
                    we = w1[0:rows, bass.ds(experts[j], 1), part, m * P:(m + 1) * P].rearrange("p e n -> p (e n)")
                    last = mm(up_bank[n % 4][:, 0:P], we, xT[0:rows, j % 3, piece],
                              start=x == 0, stop=x == len(PASSES) - 1)
                last.then_inc(up_ps, 1)

            def down(j, m):
                if m % (HM // 2) == 0:
                    pe.wait_ge(glo_ok, 2 * j + m // (HM // 2) + 1)
                if j >= 2 and m == 0:
                    pe.wait_ge(y_ok, j - 1)
                we = w2[:, bass.ds(experts[j], 1), m].rearrange("p e s n -> p (e s n)")
                mm(down_bank[j % 2][:, 0:2 * E], gs[:, j % 2, 0, m], we, start=m == 0, stop=False)
                last = mm(down_bank[j % 2][:, 0:E], gs[:, j % 2, 1, m], we[:, 0:E], start=False, stop=m == HM - 1)
                if m == HM - 1:
                    last.then_inc(down_ps, 1)

            pe.wait_ge(expert_ok, 1)
            experts = load_experts(mybir.EngineType.PE)
            pe.wait_ge(xhi_ok, TT)
            pe.wait_ge(xlo_ok, TT)
            pe.wait_ge(h2_ok, TT)
            for j in range(PICKED):
                pick(j)
            pe.wait_ge(wlo_ok, EARLY)
            for j in range(SLOT_TILES):
                pe.wait_ge(slotT_ok, 2 * (j + 1))
                if j == 1:
                    pe.wait_ge(wlo_ok, len(SPLITS))
                for m in range(HM):
                    up(j, m)
                    if j >= 1 and m >= 1:
                        down(j - 1, m - 1)
                if j >= 1:
                    down(j - 1, HM - 1)
                for n in lists_after(j):
                    slots_T(n)
            for m in range(HM):
                down(SLOT_TILES - 1, m)


_OUT = ((32, 36, 192), "float32")


def kernel(**inputs):
    import numpy as np
    import concourse.bacc as bacc
    from concourse.bass_utils import run_bass_kernel_spmd

    a = {k: np.asarray(x) for k, x in inputs.items()}
    imgs, cin, hh, ww = a["x"].shape
    ps = 16
    kdim = cin * ps * ps
    tok = imgs * (hh // ps) * (ww // ps)
    emb = a["L0_tok_proj_w"].shape[0]
    nexp, _, hid = a["L0_ffn_W1"].shape
    x = a["x"].reshape(imgs, cin, hh // ps, ps, ww // ps, ps).transpose(1, 3, 5, 0, 2, 4)
    x = x.reshape(kdim // 128, 128, tok // 128, 128).transpose(1, 2, 0, 3)
    names = ("x1", "w1", "q", "k", "a", "v", "x2", "w2")
    quant = np.concatenate([a[f"L0_attn_s{n}"].reshape(1) for n in names] +
                           [a[f"L0_attn_z{n}"].reshape(1) for n in names])

    def rows(w, r):
        return w.reshape(w.shape[0] // r, r, w.shape[1]).transpose(1, 0, 2)

    arrays = {
        "patches": x,
        "proj_w": rows(a["L0_tok_proj_w"].T, 128),
        "proj_b": a["L0_tok_proj_b"],
        "quant": quant,
        "ww1": rows(a["L0_attn_ww1"].T, emb // 2),
        "ww2": rows(a["L0_attn_ww2"].T, 128),
        "bb2": a["L0_attn_bb2"],
        "gate_w": rows(a["L0_ffn_Wg"], emb // 2),
        "gate_b": a["L0_ffn_bg"],
        "w1": a["L0_ffn_W1"].transpose(1, 0, 2),
        "b1": a["L0_ffn_b1"].reshape(nexp, hid // 128, 128).transpose(2, 0, 1),
        "w2": a["L0_ffn_W2"].reshape(nexp, hid // 128, 128, emb).transpose(2, 0, 1, 3),
        "b2": a["L0_ffn_b2"],
    }
    nc = bacc.Bacc("TRN2", target_bir_lowering=False, num_devices=1)
    args, sent = [], {}
    for name, arr in arrays.items():
        sent[f"in_{name}"] = np.ascontiguousarray(arr)
        args.append(nc.dram_tensor(f"in_{name}", arr.shape, mybir.dt.from_np(arr.dtype), kind="ExternalInput").ap())
    args.append(nc.dram_tensor("out_0", (tok, emb), F32, kind="ExternalOutput").ap())
    vit_kernel(nc, *args)
    r = run_bass_kernel_spmd(nc, [sent], core_ids=[0])
    return r.results[0]["out_0"].reshape(_OUT[0])
```
